# Optimizing a Trainium2 kernel written in Bass

```python
import numpy as np
import jax
import jax.numpy as jnp

def _softmax(x, axis=-1):
    return jax.nn.softmax(x, axis=axis)

def _gelu(x):
    return jax.nn.gelu(x, approximate=True)

def _silu(x):
    return jax.nn.silu(x)

def _sigmoid(x):
    return jax.nn.sigmoid(x)

def _layernorm(x, axis=-1, eps=1e-05):
    m = jnp.mean(x, axis=axis, keepdims=True)
    v = jnp.var(x, axis=axis, keepdims=True)
    return (x - m) / jnp.sqrt(v + eps)

def _scatter_add(tgt, idx, src, axis=0):
    return tgt.at[idx].add(src)

def _segment_sum(src, seg, n):
    return jax.ops.segment_sum(src, seg, n)
kernel_name = 'mk_hybrid_d1_jaxref_r8_7d905f'

def setup_inputs(seed: int=0):
    np.random.seed(seed)
    _w = jnp.asarray

    def _L0_attn_a_setup():
        import jax, jax.numpy as jnp
        import numpy as np
        import math
        H = 256
        NH = 16
        HD = H // NH
        THETA = 10000.0

        def rotate_half(x):
            x1, x2 = (x[..., :HD // 2], x[..., HD // 2:])
            return jnp.concatenate((-x2, x1), axis=-1)

        def rope_tables(seq_len, dtype):
            inv_freq = 1.0 / THETA ** (np.arange(0, HD, 2, dtype=np.float32) / HD)
            t = np.arange(seq_len, dtype=np.float32)
            freqs = np.einsum('i,j->ij', t, inv_freq)
            emb = np.concatenate((freqs, freqs), axis=-1)
            return (jnp.asarray(np.cos(emb), dtype), jnp.asarray(np.sin(emb), dtype))
        key = jax.random.key(seed)
        ks = jax.random.split(key, 5)
        B, S = (2, 256)
        scale = 1.0 / math.sqrt(H)
        return {'hidden_states': jax.random.normal(ks[0], (B, S, H), jnp.float32), 'Wq': jax.random.normal(ks[1], (H, H), jnp.float32) * scale, 'Wk': jax.random.normal(ks[2], (H, H), jnp.float32) * scale, 'Wv': jax.random.normal(ks[3], (H, H), jnp.float32) * scale, 'Wo': jax.random.normal(ks[4], (H, H), jnp.float32) * scale}
    _L0_attn_a_in = _L0_attn_a_setup()

    def _L0_attn_b_setup():
        import jax, jax.numpy as jnp
        import numpy as np
        NUM_HEADS = 16
        ROPE_BASE = 10000.0

        def _rope_tables(seq_len, head_dim, scaling_factor=1.0):
            inv_freq = 1.0 / ROPE_BASE ** (jnp.arange(0, head_dim, 2, dtype=jnp.float32) / head_dim)
            t = jnp.arange(seq_len, dtype=jnp.float32) * scaling_factor
            freqs = jnp.einsum('i,j->ij', t, inv_freq)
            c = jnp.sin(freqs)
            s = jnp.cos(freqs)
            return (c, s)

        def _apply_rope(x, c, s):
            x1, x2 = jnp.split(x, 2, axis=-1)
            c = c[None, None]
            s = s[None, None]
            return jnp.concatenate([x1 * c - x2 * s, x1 * s + x2 * c], axis=-1)
        key = jax.random.key(seed)
        ks = jax.random.split(key, 5)
        B, S, H = (4, 256, 256)
        x = jax.random.normal(ks[0], (B, S, H), dtype=jnp.float32)
        scale = 1.0 / np.sqrt(H)
        Wq = jax.random.normal(ks[1], (H, H), dtype=jnp.float32) * scale
        Wk = jax.random.normal(ks[2], (H, H), dtype=jnp.float32) * scale
        Wv = jax.random.normal(ks[3], (H, H), dtype=jnp.float32) * scale
        Wo = jax.random.normal(ks[4], (H, H), dtype=jnp.float32) * scale
        return {'x': x, 'Wq': Wq, 'Wk': Wk, 'Wv': Wv, 'Wo': Wo}
    _L0_attn_b_in = _L0_attn_b_setup()

    def _L0_ffn_setup():
        import jax, jax.numpy as jnp
        import numpy as np
        H = 256
        I = 176
        E = 16
        K = 2
        N_SHARED = 2
        IS = I * N_SHARED
        ROUTED_SCALE = 1.0
        CAPACITY = 128

        def _moe_forward(hidden_states, gate_w, w_gate, w_up, w_down, ws_gate, ws_up, ws_down):
            B, S, _ = hidden_states.shape
            x = hidden_states.reshape(-1, H)
            T = x.shape[0]
            logits = jnp.einsum('th,eh->te', x.astype(jnp.float32), gate_w.astype(jnp.float32))
            scores = jax.nn.softmax(logits, axis=-1)
            topk_w, topk_idx = jax.lax.top_k(scores, K)
            topk_w = (topk_w * ROUTED_SCALE).astype(x.dtype)
            flat_idx = topk_idx.reshape(-1)
            order = jnp.argsort(flat_idx)
            sorted_e = flat_idx[order]
            sorted_t = order // K
            counts = jnp.bincount(flat_idx, length=E)
            starts = jnp.cumsum(counts) - counts
            pos = jnp.arange(T * K) - starts[sorted_e]
            buf = jnp.zeros((E, CAPACITY, H), x.dtype).at[sorted_e, pos].set(x[sorted_t], mode='drop')
            g = jax.nn.silu(jnp.einsum('ech,ehi->eci', buf, w_gate))
            u = jnp.einsum('ech,ehi->eci', buf, w_up)
            expert_out = jnp.einsum('eci,eih->ech', g * u, w_down)
            gathered = expert_out[sorted_e, pos]
            out_flat = jnp.zeros((T * K, H), x.dtype).at[order].set(gathered)
            y = (out_flat.reshape(T, K, H) * topk_w[..., None]).sum(axis=1)
            sh = jnp.einsum('ti,ih->th', jax.nn.silu(x @ ws_gate) * (x @ ws_up), ws_down)
            return (y + sh).reshape(B, S, H)
        key = jax.random.key(seed)
        ks = jax.random.split(key, 8)
        B, S = (2, 128)
        scale = 0.02
        return {'hidden_states': jax.random.normal(ks[0], (B, S, H), jnp.float32), 'gate_w': jax.random.normal(ks[1], (E, H), jnp.float32) * scale, 'w_gate': jax.random.normal(ks[2], (E, H, I), jnp.float32) * scale, 'w_up': jax.random.normal(ks[3], (E, H, I), jnp.float32) * scale, 'w_down': jax.random.normal(ks[4], (E, I, H), jnp.float32) * scale, 'ws_gate': jax.random.normal(ks[5], (H, IS), jnp.float32) * scale, 'ws_up': jax.random.normal(ks[6], (H, IS), jnp.float32) * scale, 'ws_down': jax.random.normal(ks[7], (IS, H), jnp.float32) * scale}
    _L0_ffn_in = _L0_ffn_setup()
    _d = {'L0_attn_a_hidden_states': _L0_attn_a_in['hidden_states'], 'L0_attn_a_Wq': _L0_attn_a_in['Wq'], 'L0_attn_a_Wk': _L0_attn_a_in['Wk'], 'L0_attn_a_Wv': _L0_attn_a_in['Wv'], 'L0_attn_a_Wo': _L0_attn_a_in['Wo'], 'L0_attn_b_Wq': _L0_attn_b_in['Wq'], 'L0_attn_b_Wk': _L0_attn_b_in['Wk'], 'L0_attn_b_Wv': _L0_attn_b_in['Wv'], 'L0_attn_b_Wo': _L0_attn_b_in['Wo'], 'L0_ffn_gate_w': _L0_ffn_in['gate_w'], 'L0_ffn_w_gate': _L0_ffn_in['w_gate'], 'L0_ffn_w_up': _L0_ffn_in['w_up'], 'L0_ffn_w_down': _L0_ffn_in['w_down'], 'L0_ffn_ws_gate': _L0_ffn_in['ws_gate'], 'L0_ffn_ws_up': _L0_ffn_in['ws_up'], 'L0_ffn_ws_down': _L0_ffn_in['ws_down']}
    _x0 = _d['L0_attn_a_hidden_states']
    _d['L0_attn_a_hidden_states'] = jax.random.normal(jax.random.fold_in(jax.random.key(seed), 1), (1, 1024, 256), dtype=_x0.dtype)
    del _x0
    return _d

def reference(L0_attn_a_hidden_states, L0_attn_a_Wq, L0_attn_a_Wk, L0_attn_a_Wv, L0_attn_a_Wo, L0_attn_b_Wq, L0_attn_b_Wk, L0_attn_b_Wv, L0_attn_b_Wo, L0_ffn_gate_w, L0_ffn_w_gate, L0_ffn_w_up, L0_ffn_w_down, L0_ffn_ws_gate, L0_ffn_ws_up, L0_ffn_ws_down):

    def _L0_attn_a_ref(hidden_states, Wq, Wk, Wv, Wo):
        import jax, jax.numpy as jnp
        import numpy as np
        import math
        H = 256
        NH = 16
        HD = H // NH
        THETA = 10000.0

        def rotate_half(x):
            x1, x2 = (x[..., :HD // 2], x[..., HD // 2:])
            return jnp.concatenate((-x2, x1), axis=-1)

        def rope_tables(seq_len, dtype):
            inv_freq = 1.0 / THETA ** (np.arange(0, HD, 2, dtype=np.float32) / HD)
            t = np.arange(seq_len, dtype=np.float32)
            freqs = np.einsum('i,j->ij', t, inv_freq)
            emb = np.concatenate((freqs, freqs), axis=-1)
            return (jnp.asarray(np.cos(emb), dtype), jnp.asarray(np.sin(emb), dtype))
        B, S, _ = hidden_states.shape

        def proj(W):
            y = jnp.einsum('bsh,oh->bso', hidden_states, W)
            return y.reshape(B, S, NH, HD).transpose(0, 2, 1, 3)
        q, k, v = (proj(Wq), proj(Wk), proj(Wv))
        cos, sin = rope_tables(S, hidden_states.dtype)
        cos, sin = (cos[None, None], sin[None, None])
        q = q * cos + rotate_half(q) * sin
        k = k * cos + rotate_half(k) * sin
        scores = jnp.einsum('bhqd,bhkd->bhqk', q, k) / math.sqrt(HD)
        causal = jnp.triu(jnp.ones((S, S), bool), k=1)
        scores = jnp.where(causal, -jnp.inf, scores)
        attn = jax.nn.softmax(scores, axis=-1)
        out = jnp.einsum('bhqk,bhkd->bhqd', attn, v)
        out = out.transpose(0, 2, 1, 3).reshape(B, S, H)
        return jnp.einsum('bsh,oh->bso', out, Wo)

    def _L0_attn_b_ref(x, Wq, Wk, Wv, Wo):
        import jax, jax.numpy as jnp
        import numpy as np
        NUM_HEADS = 16
        ROPE_BASE = 10000.0

        def _rope_tables(seq_len, head_dim, scaling_factor=1.0):
            inv_freq = 1.0 / ROPE_BASE ** (jnp.arange(0, head_dim, 2, dtype=jnp.float32) / head_dim)
            t = jnp.arange(seq_len, dtype=jnp.float32) * scaling_factor
            freqs = jnp.einsum('i,j->ij', t, inv_freq)
            c = jnp.sin(freqs)
            s = jnp.cos(freqs)
            return (c, s)

        def _apply_rope(x, c, s):
            x1, x2 = jnp.split(x, 2, axis=-1)
            c = c[None, None]
            s = s[None, None]
            return jnp.concatenate([x1 * c - x2 * s, x1 * s + x2 * c], axis=-1)
        B, S, H = x.shape
        nh = NUM_HEADS
        hd = H // nh
        scale = hd ** (-0.5)

        def proj(W):
            y = jnp.einsum('bsi,oi->bso', x, W)
            return y.reshape(B, S, nh, hd).transpose(0, 2, 1, 3)
        Q = proj(Wq)
        K = proj(Wk)
        V = proj(Wv)
        c, s = _rope_tables(S, hd)
        Q = _apply_rope(Q, c, s)
        K = _apply_rope(K, c, s)
        scores = jnp.einsum('bhqd,bhkd->bhqk', Q, K) * scale
        mask = jnp.tril(jnp.ones((S, S), dtype=bool))
        scores = jnp.where(mask[None, None], scores, -jnp.inf)
        attn = jax.nn.softmax(scores, axis=-1)
        out = jnp.einsum('bhqk,bhkd->bhqd', attn, V)
        out = out.transpose(0, 2, 1, 3).reshape(B, S, H)
        return jnp.einsum('bsi,oi->bso', out, Wo)

    def _L0_ffn_ref(hidden_states, gate_w, w_gate, w_up, w_down, ws_gate, ws_up, ws_down):
        import jax, jax.numpy as jnp
        import numpy as np
        H = 256
        I = 176
        E = 16
        K = 2
        N_SHARED = 2
        IS = I * N_SHARED
        ROUTED_SCALE = 1.0
        CAPACITY = 128

        def _moe_forward(hidden_states, gate_w, w_gate, w_up, w_down, ws_gate, ws_up, ws_down):
            B, S, _ = hidden_states.shape
            x = hidden_states.reshape(-1, H)
            T = x.shape[0]
            logits = jnp.einsum('th,eh->te', x.astype(jnp.float32), gate_w.astype(jnp.float32))
            scores = jax.nn.softmax(logits, axis=-1)
            topk_w, topk_idx = jax.lax.top_k(scores, K)
            topk_w = (topk_w * ROUTED_SCALE).astype(x.dtype)
            flat_idx = topk_idx.reshape(-1)
            order = jnp.argsort(flat_idx)
            sorted_e = flat_idx[order]
            sorted_t = order // K
            counts = jnp.bincount(flat_idx, length=E)
            starts = jnp.cumsum(counts) - counts
            pos = jnp.arange(T * K) - starts[sorted_e]
            buf = jnp.zeros((E, CAPACITY, H), x.dtype).at[sorted_e, pos].set(x[sorted_t], mode='drop')
            g = jax.nn.silu(jnp.einsum('ech,ehi->eci', buf, w_gate))
            u = jnp.einsum('ech,ehi->eci', buf, w_up)
            expert_out = jnp.einsum('eci,eih->ech', g * u, w_down)
            gathered = expert_out[sorted_e, pos]
            out_flat = jnp.zeros((T * K, H), x.dtype).at[order].set(gathered)
            y = (out_flat.reshape(T, K, H) * topk_w[..., None]).sum(axis=1)
            sh = jnp.einsum('ti,ih->th', jax.nn.silu(x @ ws_gate) * (x @ ws_up), ws_down)
            return (y + sh).reshape(B, S, H)
        return _moe_forward(hidden_states, gate_w, w_gate, w_up, w_down, ws_gate, ws_up, ws_down)
    x = L0_attn_a_hidden_states
    x = x + _L0_attn_a_ref(_layernorm(x, axis=-1), L0_attn_a_Wq, L0_attn_a_Wk, L0_attn_a_Wv, L0_attn_a_Wo)
    x = x + _L0_ffn_ref(_layernorm(x, axis=-1), L0_ffn_gate_w, L0_ffn_w_gate, L0_ffn_w_up, L0_ffn_w_down, L0_ffn_ws_gate, L0_ffn_ws_up, L0_ffn_ws_down)
    x = x + _L0_attn_b_ref(_layernorm(x, axis=-1), L0_attn_b_Wq, L0_attn_b_Wk, L0_attn_b_Wv, L0_attn_b_Wo)
    x = x + _L0_ffn_ref(_layernorm(x, axis=-1), L0_ffn_gate_w, L0_ffn_w_gate, L0_ffn_w_up, L0_ffn_w_down, L0_ffn_ws_gate, L0_ffn_ws_up, L0_ffn_ws_down)
    return x

_drawn_inputs = setup_inputs


def setup_inputs(seed=0):
    import zlib

    import numpy as np

    out = dict(_drawn_inputs(seed))
    spreads = {}
    factors = {'L0_ffn_gate_w': 8.0, 'L0_ffn_w_gate': 8.0, 'L0_ffn_w_up': 8.0, 'L0_ffn_w_down': 8.0}
    for name, (base, spread) in spreads.items():
        noise = np.random.default_rng([zlib.crc32(name.encode()), seed]).standard_normal(out[name].shape)
        drawn = base * np.exp(spread * noise) if base else spread * noise
        out[name] = jnp.asarray(drawn.astype(out[name].dtype))
    for name, factor in factors.items():
        out[name] = (out[name] * factor).astype(out[name].dtype)
    return out
```

```python
import numpy as np
from contextlib import ExitStack

import concourse.bass as bass
from concourse import mybir

F32 = mybir.dt.float32
BF16 = mybir.dt.bfloat16
U32 = mybir.dt.uint32
ALU = mybir.AluOpType
ACT = mybir.ActivationFunctionType
AX = mybir.AxisListType

P = 128
S = 1024
NT = S // P
H = 256
KT = H // P
NH = 16
HD = H // NH
HH = HD // 2
LAYERS = 2
GH = 4
NG = NH // GH
PARTS = 3
NB = 6
SR = NB * HD
SA = SR + PARTS
VW = 32
HALF = 512
NQ = S // HALF
E = 16
CAP = 128
TOPK = 2
I = 176
IH = I // 2
IS = 352
IS_TILES = [(0, 128), (128, 128), (256, 96)]
EPS = 1e-5
NEG = -3.0e38
LAST_MASKED = HALF - P

STEPS = [(0, 0), (0, 1), (0, 2), (0, 3), (1, 0), (1, 4), (1, 5), (1, 6), (1, 7), (1, 1), (1, 2), (1, 3)]
NS = len(STEPS)
STEP_ENDS = {3: 0, 11: 1}
UNITS = []
for j in range(GH):
    for t in range(NT):
        keys = (t + 1) * P
        if keys > HALF:
            UNITS.append((j, t, 0, HALF, False))
            UNITS.append((j, t, HALF, keys - HALF, True))
        else:
            UNITS.append((j, t, 0, keys, True))
NU = len(UNITS)
UNITS_A_STEP = 5
MAX_STEP = 10


def diagonal(step):
    qc, kt = step
    return kt * P >= qc * HALF


DIAGONALS = sum(diagonal(s) for s in STEPS)


def columns(step):
    qc, kt = step
    first = max(kt * P - qc * HALF, 0)
    return first, HALF - first


def units_of(step):
    return range(min(step * UNITS_A_STEP, NU), min((step + 1) * UNITS_A_STEP, NU))


def build(nc, x, wqkv, wo, gate, wgu, wdown, wsgu, wsdown, rope, out):
    ctx = ExitStack()
    with ctx:
        def sb(name, shape, dt=F32):
            return ctx.enter_context(nc.sbuf_tensor(name, shape, dt))

        def sem(name):
            return ctx.enter_context(nc.semaphore(name))

        x_sb = sb("x_sb", [P, NT, H])
        norms = sb("norms", [P, 2 * NT * H])
        xn = norms[:, 0:NT * H].rearrange("p (t d) -> p t d", t=NT)
        xnT = norms[:, NT * H:2 * NT * H].rearrange("p (k s) -> p k s", k=KT)
        oT = norms[:, :].rearrange("p (g s) -> p g s", g=NG)
        QW, VWORDS = NH * S // 2, NT * NH * VW
        arena = sb("arena", [P, 2 * QW + VWORDS])
        q_st = arena[:, 0:QW].bitcast(BF16).rearrange("p (h s) -> p h s", h=NH)
        k_st = arena[:, QW:2 * QW].bitcast(BF16).rearrange("p (h s) -> p h s", h=NH)
        v_x = arena[:, 2 * QW:].rearrange("p (t h w) -> p t h w", t=NT, h=NH)
        GUW, EW = KT * 2 * I, KT * 2 * I + 2 * H
        experts = arena[:, 0:E * EW].rearrange("p (e w) -> p e w", e=E)
        wgu_sb = experts[:, :, 0:GUW].rearrange("p e (k n) -> p e k n", k=KT)
        wd_sb = experts[0:IH, :, GUW:EW].rearrange("p e (k n) -> p e k n", k=2)
        stage = sb("stage", [P, 6144])
        rope_a = [stage[:, 1024 * b:1024 * b + 512] for b in range(2)]
        rope_b = [stage[:, 1024 * b + 512:1024 * b + 1024] for b in range(2)]
        roped = [stage[:, 2048 + 512 * b:2560 + 512 * b] for b in range(2)]
        stacks = [stage[:, 3072 + 1536 * b:4608 + 1536 * b].bitcast(BF16)
                  .rearrange("p (h j d) -> p h j d", h=2 * NH, j=NB) for b in range(2)]
        gathered = stage[:, 0:TOPK * NT * H].rearrange("p (k t d) -> p k t d", k=TOPK, t=NT)
        silu_s = [stage[:, 4096 + 512 * b:4608 + 512 * b] for b in range(2)]
        eo = [stage[:, 5120 + 256 * b:5376 + 256 * b] for b in range(4)]
        probs_all = sb("probs", [P, 4 * 2 * HALF])
        probs = [probs_all[:, 1024 * b:1024 * b + 1024].rearrange("p (j n) -> p j n", j=2) for b in range(4)]
        slots = probs_all[:, :].rearrange("p (e d) -> p e d", e=E)
        wqkv_sb = sb("wqkv_sb", [P, KT, 3 * H])
        wo_sb = sb("wo_sb", [P, LAYERS, KT, H])
        gate_sb = sb("gate_sb", [P, KT, E])
        wsgu_sb = sb("wsgu_sb", [P, KT, 2 * IS])
        wsd_sb = sb("wsd_sb", [P, 3, H])
        rope_sb = sb("rope_sb", [P, LAYERS, NT, 2, HD])
        ident = sb("ident", [P, P])
        ident_b = sb("ident_b", [P, P], BF16)
        before = sb("before", [P, P], BF16)
        ones_b = sb("ones_b", [P, P], BF16)
        mask = sb("mask", [P, HALF])
        revio = sb("revio", [P, 1, E])
        revio_i = sb("revio_i", [P, E], mybir.dt.int32)
        neghalf = sb("neghalf", [P, NT])
        stats = sb("stats", [P, NT, 6])
        meanvar = sb("meanvar", [P, NT, 2])
        vareps = sb("vareps", [P, NT])
        rstd = sb("rstd", [P, NT])
        dump = sb("dump", [P, 2, HALF], BF16)
        rowmax = sb("rowmax", [P, GH, NT])
        rowmax_a = sb("rowmax_a", [P, GH, NT // 2])
        negmax = sb("negmax", [GH * NT, P])
        negrest = sb("negrest", [GH * NT, P])
        shift = sb("shift", [GH * NT, PARTS, P], BF16)
        recip = sb("recip", [P, 2, NH])
        o_tok = sb("o_tok", [P, 2, H])
        o_T = sb("o_T", [P, 2, KT, P])
        hsT = sb("hsT", [P, 3, S])
        slotsT = sb("slotsT", [P, 2, KT, P])
        silu_e = sb("silu_e", [P, 2, I])
        h_e = sb("h_e", [P, 2, I])
        hT_e = sb("hT_e", [IH, 2, 2, P])
        lg = sb("lg", [P, NT, E])
        ex = sb("ex", [P, NT, E])
        sc = sb("sc", [P, NT, E])
        tmp = sb("tmp", [P, NT, E])
        hot = sb("hot", [P, TOPK, NT, E])
        hot_b = sb("hot_b", [P, NT, E], BF16)
        s8 = sb("s8", [P, 2, NT])
        topw = sb("topw", [P, TOPK, NT])
        key = sb("key", [P, TOPK, NT])
        rank = sb("rank", [P, TOPK, NT])
        slot0 = sb("slot0", [P, TOPK, NT])
        slot1 = sb("slot1", [P, TOPK, NT])
        slot2 = sb("slot2", [P, TOPK, NT])
        put_at = sb("put_at", [P, TOPK, NT], U32)
        get_at = sb("get_at", [P, TOPK, NT], U32)
        zeros = o_tok[:, :, :]

        slots_dram = nc.dram_tensor("slots_dram", (E * CAP, H), F32, kind="Internal").ap()
        eo_dram = nc.dram_tensor("eo_dram", (E * CAP, H), F32, kind="Internal").ap()

        banks = ctx.enter_context(nc.psum_tensor("banks", [P, 8, HALF], F32))

        def bank(n):
            return banks[:, n, :]

        x_loaded = [sem(f"x_loaded{t}") for t in range(NT)]
        wqkv_loaded = sem("wqkv_loaded")
        wo_loaded = sem("wo_loaded")
        rope_loaded = sem("rope_loaded")
        moe_loaded = sem("moe_loaded")
        consts_ready = sem("consts_ready")
        mask_ready = sem("mask_ready")
        zeros_ready = sem("zeros_ready")
        slots_zeroed = sem("slots_zeroed")
        vareps_ready = sem("vareps_ready")
        rstd_ready = sem("rstd_ready")
        xn_ready = sem("xn_ready")
        xT_done = sem("xT_done")
        xnT_ready = sem("xnT_ready")
        proj_done = sem("proj_done")
        rope_mul = sem("rope_mul")
        rope_sum = sem("rope_sum")
        part1_ready = sem("part1_ready")
        rest_ready = sem("rest_ready")
        part2_ready = sem("part2_ready")
        stack_ready = sem("stack_ready")
        stackT_done = sem("stackT_done")
        stackT_read_v = sem("stackT_read_v")
        stackT_read_a = sem("stackT_read_a")
        v_copied = sem("v_copied")
        arena_fixed = sem("arena_fixed")
        s1_done = sem("s1_done")
        s1_read = sem("s1_read")
        max_ready = sem("max_ready")
        maxT_done = sem("maxT_done")
        negmax_ready = sem("negmax_ready")
        shift_ready = sem("shift_ready")
        shift_loaded = sem("shift_loaded")
        s2_done = sem("s2_done")
        exp_done = sem("exp_done")
        masked = sem("masked")
        pv_done = sem("pv_done")
        oT_ready = sem("oT_ready")
        oback_done = sem("oback_done")
        o_ready = sem("o_ready")
        o2T_done = sem("o2T_done")
        o_T_ready = sem("o_T_ready")
        wo_done = sem("wo_done")
        attn_added = sem("attn_added")
        logits_done = sem("logits_done")
        logits_read = sem("logits_read")
        exp_in = sem("exp_in")
        exp_out = sem("exp_out")
        hot_ready = sem("hot_ready")
        rank_done = sem("rank_done")
        rank_read = sem("rank_read")
        slots_known = sem("slots_known")
        scattered = sem("scattered")
        slots_loaded = [sem(f"slots_loaded{n}") for n in range(4)]
        shared_up = sem("shared_up")
        shared_silu = sem("shared_silu")
        shared_h = sem("shared_h")
        shared_down = sem("shared_down")
        shared_added = sem("shared_added")
        expert_loaded = [sem(f"expert_loaded{e}") for e in range(E)]
        slotT_done = sem("slotT_done")
        slotT_ready = sem("slotT_ready")
        gu_done = sem("gu_done")
        silu_done = sem("silu_done")
        h_ready = sem("h_ready")
        hT_done = sem("hT_done")
        hT_ready = sem("hT_ready")
        down_done = sem("down_done")
        eo_ready = sem("eo_ready")
        eo_stored = [sem(f"eo_stored{n}") for n in range(4)]
        got = [sem(f"got{t}") for t in range(NT)]
        layer_done = sem("layer_done")
        out_stored = sem("out_stored")
        dve_step = sem("dve_step")
        pool_step = sem("pool_step")

        block = ctx.enter_context(nc.Block())

        @block.sync
        def _(sp):
            for t in range(NT):
                sp.dma_start(x_sb[:, t, :], x[t * P:(t + 1) * P, :]).then_inc(x_loaded[t], 16)
            sp.dma_start(wqkv_sb[:, :, :], wqkv[0].rearrange("(k p) n -> p k n", p=P)).then_inc(wqkv_loaded, 16)
            sp.dma_start(rope_sb[:, :, :, :, :], rope.rearrange("p l t m d -> p l t m d")).then_inc(rope_loaded, 16)
            sp.dma_start(wo_sb[:, :, :, :], wo.rearrange("l (k p) n -> p l k n", p=P)).then_inc(wo_loaded, 16)
            sp.dma_start(gate_sb[:, :, :], gate.rearrange("(k p) e -> p k e", p=P)).then_inc(moe_loaded, 16)
            sp.dma_start(wsgu_sb[:, :, :], wsgu.rearrange("(k p) n -> p k n", p=P)).then_inc(moe_loaded, 16)
            sp.dma_start(wsd_sb[:, 0:2, :], wsdown[0:2 * P, :].rearrange("(k p) n -> p k n", p=P)).then_inc(moe_loaded, 16)
            sp.dma_start(wsd_sb[0:IS - 2 * P, 2, :], wsdown[2 * P:IS, :]).then_inc(moe_loaded, 16)
            sp.wait_ge(zeros_ready, 1)
            for n in range(8):
                sp.dma_start(slots_dram[n * 2 * P:(n + 1) * 2 * P, :].rearrange("(k p) d -> p k d", p=P),
                             zeros).then_inc(slots_zeroed, 16)
            for l in range(LAYERS):
                if l > 0:
                    sp.wait_ge(proj_done, NT * l)
                    sp.dma_start(wqkv_sb[:, :, :], wqkv[l].rearrange("(k p) n -> p k n", p=P)).then_inc(wqkv_loaded, 16)
                for g in range(NG):
                    sp.wait_ge(shift_ready, l * NG + g + 1)
                    for part in range(PARTS):
                        sp.dma_start(q_st[SR + part:SR + part + 1, GH * g:GH * g + GH, :],
                                     shift[:, part, :]).then_inc(shift_loaded, 16)
                sp.wait_ge(pv_done, (l + 1) * NG * NS)
                for e in range(E):
                    sp.dma_start(wgu_sb[:, e, :, :], wgu[e].rearrange("(k p) n -> p k n", p=P)).then_inc(expert_loaded[e], 16)
                    sp.dma_start(wd_sb[:, e, :, :], wdown[e].rearrange("(k p) n -> p k n", p=IH)).then_inc(expert_loaded[e], 16)
                sp.wait_ge(scattered, (l + 1) * TOPK * NT * 16)
                for n in range(4):
                    sp.dma_start(slots[:, 4 * n:4 * n + 4, :],
                                 slots_dram[n * 4 * P:(n + 1) * 4 * P, :].rearrange("(e p) d -> p e d", p=P)
                                 ).then_inc(slots_loaded[n], 16)
                for e in range(E):
                    sp.wait_ge(eo_ready, l * E + e + 1)
                    sp.dma_start(eo_dram[e * CAP:(e + 1) * CAP, :], eo[e % 4]).then_inc(eo_stored[e % 4], 16)
            for t in range(NT):
                sp.wait_ge(layer_done, (LAYERS - 1) * NT + t + 1)
                sp.dma_start(out[t * P:(t + 1) * P, :], x_sb[:, t, :]).then_inc(out_stored, 16)
            sp.wait_ge(out_stored, 16 * NT)

        @block.gpsimd
        def _(pool):
            steps = [0]

            def settle(ins):
                steps[0] += 1
                ins.then_inc(pool_step, 1)
                pool.wait_ge(pool_step, steps[0])

            nc.gpsimd.memset(neghalf[:, :], -0.5)
            nc.gpsimd.memset(zeros, 0.0).then_inc(zeros_ready, 1)
            nc.gpsimd.memset(ident[:, :], 0.0)
            nc.gpsimd.memset(before[:, :], 1.0)
            nc.gpsimd.memset(ones_b[:, :], 1.0)
            nc.gpsimd.iota(revio_i[:, :], pattern=[[-1, E]], base=E, channel_multiplier=0)
            settle(nc.gpsimd.memset(mask[:, :], 0.0))
            nc.gpsimd.tensor_copy(revio[:, 0, :], revio_i[:, :])
            settle(nc.gpsimd.affine_select(out=ident[:, :], in_=ident[:, :], compare_op=ALU.not_equal, fill=1.0,
                                           base=0, pattern=[[-1, P]], channel_multiplier=1))
            nc.gpsimd.tensor_copy(ident_b[:, :], ident[:, :])
            nc.gpsimd.affine_select(out=before[:, :], in_=before[:, :], compare_op=ALU.is_gt, fill=0.0,
                                    base=0, pattern=[[1, P]], channel_multiplier=-1).then_inc(consts_ready, 1)
            nc.gpsimd.affine_select(out=mask[:, LAST_MASKED:HALF], in_=mask[:, LAST_MASKED:HALF],
                                    compare_op=ALU.is_ge, fill=NEG, base=0, pattern=[[-1, P]],
                                    channel_multiplier=1).then_inc(mask_ready, 1)

            def norm(n):
                pool.wait_ge(vareps_ready, n + 1)
                nc.gpsimd.tensor_tensor(rstd[:, :], vareps[:, :], neghalf[:, :], ALU.pow).then_inc(rstd_ready, 1)

            def causal(l, g, s):
                n, (qc, kt) = (l * NG + g) * NS + s, STEPS[s]
                if diagonal(STEPS[s]):
                    for pair in range(2):
                        u = 2 * n + pair
                        pool.wait_ge(exp_done, u + 1)
                        block_p = probs[u % 4][:, :, 0:P]
                        nc.gpsimd.affine_select(out=block_p, in_=block_p, compare_op=ALU.is_ge, fill=0.0, base=0,
                                                pattern=[[0, 2], [1, P]], channel_multiplier=-1).then_inc(masked, 1)

            def split_max(l, g):
                n = l * NG + g
                pool.wait_ge(negmax_ready, n + 1)
                if n:
                    pool.wait_ge(shift_loaded, 16 * PARTS * n)
                settle(nc.gpsimd.tensor_copy(shift[:, 0, :], negmax[:, :]))
                settle(nc.gpsimd.tensor_tensor(negrest[:, :], negmax[:, :], shift[:, 0, :], ALU.subtract))
                settle(nc.gpsimd.tensor_copy(shift[:, 1, :], negrest[:, :]))
                nc.gpsimd.tensor_tensor(shift[:, 2, :], negrest[:, :], shift[:, 1, :], ALU.subtract).then_inc(shift_ready, 1)

            for l in range(LAYERS):
                norm(2 * l)
                if l > 0:
                    pool.wait_ge(down_done, l * E)
                pool.wait_ge(rstd_ready, 2 * l + 1)
                settle(nc.gpsimd.memset(k_st[SR:SA, :, :], 1.0))
                nc.gpsimd.memset(v_x[:, :, :, HD + 1:VW], 0.0)
                nc.gpsimd.memset(v_x[:, :, :, HD:HD + 1], 1.0).then_inc(arena_fixed, 1)
                for t in range(NT + 1):
                    if t < NT:
                        i = l * NT + t
                        pool.wait_ge(rope_mul, i + 1)
                        if i >= 2:
                            pool.wait_ge(stack_ready, i - 1)
                        nc.gpsimd.tensor_tensor(roped[i % 2], rope_a[i % 2], rope_b[i % 2], ALU.add).then_inc(rope_sum, 1)
                    if t > 0:
                        i = l * NT + t - 1
                        pool.wait_ge(part2_ready, i + 1)
                        b, st = roped[i % 2].rearrange("p (h d) -> p h d", h=2 * NH), stacks[i % 2]
                        nc.gpsimd.tensor_tensor(st[:, 0:NH, 5, :], b[:, 0:NH, :], st[:, 0:NH, 1, :], ALU.subtract)
                        nc.gpsimd.tensor_tensor(st[:, NH:2 * NH, 2, :], b[:, NH:2 * NH, :], st[:, NH:2 * NH, 1, :],
                                                ALU.subtract).then_inc(stack_ready, 1)
                split_max(l, 0)
                for g in range(NG):
                    for s in range(NS):
                        if s == MAX_STEP and g + 1 < NG:
                            split_max(l, g + 1)
                        causal(l, g, s)
                norm(2 * l + 1)
                pool.wait_ge(slots_known, l + 1)
                if l == 0:
                    pool.wait_ge(slots_zeroed, 16 * 8)
                else:
                    for n in range(4):
                        pool.wait_ge(slots_loaded[n], 16 * l)
                for t in range(NT):
                    for k in range(TOPK):
                        nc.gpsimd.indirect_dma_start(
                            out=slots_dram, out_offset=bass.IndirectOffsetOnAxis(ap=put_at[:, k, t:t + 1], axis=0),
                            in_=xn[:, t, :], in_offset=None, bounds_check=E * CAP - 1, oob_is_err=False
                        ).then_inc(scattered, 16)
                for n in range(4):
                    pool.wait_ge(eo_stored[n], 16 * (l + 1) * E // 4)
                for t in range(NT):
                    for k in range(TOPK):
                        nc.gpsimd.indirect_dma_start(
                            out=gathered[:, k, t, :], out_offset=None, in_=eo_dram,
                            in_offset=bass.IndirectOffsetOnAxis(ap=get_at[:, k, t:t + 1], axis=0)
                        ).then_inc(got[t], 16)

        @block.scalar
        def _(act):
            def copy_xT(n, t):
                i = n * NT + t
                act.wait_ge(xT_done, i + 1)
                nc.scalar.copy(xnT[:, :, t * P:(t + 1) * P],
                               bank(4 + i % 2)[:, 0:H].rearrange("p (k s) -> p k s", k=KT)).then_inc(xnT_ready, 1)

            def exps(l, g, s):
                n = (l * NG + g) * NS + s
                first, width = columns(STEPS[s])
                if n >= 2:
                    act.wait_ge(pv_done, n - 1)
                for pair in range(2):
                    u = 2 * n + pair
                    act.wait_ge(s2_done, u + 1)
                    nc.scalar.activation(probs[u % 4][:, :, 0:width], banks[:, 2 + 2 * (u % 2):4 + 2 * (u % 2), 0:width],
                                         ACT.Exp, scale=HD ** -0.5).then_inc(exp_done, 1)

            def copy_oT(l, g, qc):
                w = (l * NG + g) * NQ + qc
                act.wait_ge(pv_done, (l * NG + g) * NS + [s for s in STEP_ENDS if STEP_ENDS[s] == qc][0] + 1)
                nc.scalar.copy(oT[:, g, qc * HALF:(qc + 1) * HALF], bank(6 + w % 2)).then_inc(oT_ready, 1)

            def negate_max(l, g):
                n = l * NG + g
                act.wait_ge(maxT_done, n + 1)
                if n:
                    act.wait_ge(shift_ready, n)
                nc.scalar.mul(negmax[:, :], bank(0)[0:GH * NT, 0:P], -1.0).then_inc(negmax_ready, 1)

            for l in range(LAYERS):
                act.wait_ge(arena_fixed, l + 1)
                for t in range(NT + 2):
                    if t < NT:
                        copy_xT(2 * l, t)
                        i = l * NT + t
                        act.wait_ge(proj_done, i + 1)
                        nc.scalar.copy(v_x[:, t, :, 0:HD],
                                       bank(2 + i % 2)[:, 0:H].rearrange("p (h d) -> p h d", h=NH)).then_inc(v_copied, 1)
                        act.wait_ge(rope_sum, i + 1)
                        if i >= 2:
                            act.wait_ge(stackT_done, 4 * (i - 1))
                        r = roped[i % 2].rearrange("p (h j d) -> p h j d", h=2 * NH, j=1)
                        st = stacks[i % 2]
                        nc.scalar.copy(st[:, 0:NH, 0:5:2, :], r[:, 0:NH].to_broadcast([P, NH, 3, HD]))
                        nc.scalar.copy(st[:, NH:2 * NH, 3:6, :],
                                       r[:, NH:2 * NH].to_broadcast([P, NH, 3, HD])).then_inc(part1_ready, 1)
                    if 0 < t <= NT:
                        i = l * NT + t - 1
                        act.wait_ge(rest_ready, i + 1)
                        r = roped[i % 2].rearrange("p (h j d) -> p h j d", h=2 * NH, j=1)
                        st = stacks[i % 2]
                        nc.scalar.copy(st[:, 0:NH, 1:4:2, :], r[:, 0:NH].to_broadcast([P, NH, 2, HD]))
                        nc.scalar.copy(st[:, NH:2 * NH, 0:2, :],
                                       r[:, NH:2 * NH].to_broadcast([P, NH, 2, HD])).then_inc(part2_ready, 1)
                    if t > 1:
                        i = l * NT + t - 2
                        act.wait_ge(stackT_done, 4 * i + 4)
                        nc.scalar.copy(k_st[0:SR, 8:16, (t - 2) * P:(t - 1) * P],
                                       bank(7)[0:SR, :].bitcast(BF16).rearrange("p (h s) -> p h s", h=8)
                                       ).then_inc(stackT_read_a, 1)
                negate_max(l, 0)
                for g in range(NG):
                    for s in range(NS):
                        if s == MAX_STEP and g + 1 < NG:
                            negate_max(l, g + 1)
                        exps(l, g, s)
                        if s - 1 in STEP_ENDS:
                            copy_oT(l, g, STEP_ENDS[s - 1])
                        if s == 0 and g > 0:
                            copy_oT(l, g - 1, 1)
                copy_oT(l, NG - 1, 1)
                for t in range(NT):
                    i = l * NT + t
                    act.wait_ge(o2T_done, i + 1)
                    if i >= 2:
                        act.wait_ge(wo_done, i - 1)
                    nc.scalar.copy(o_T[:, i % 2], bank(2 + i % 2)[:, 0:H].rearrange("p (k s) -> p k s", k=KT)
                                   ).then_inc(o_T_ready, 1)
                for t in range(NT):
                    copy_xT(2 * l + 1, t)
                act.wait_ge(exp_in, l + 1)
                nc.scalar.activation(ex[:, :, :], tmp[:, :, :], ACT.Exp).then_inc(exp_out, 1)
                for m in range(6):
                    i, (_, mw) = 6 * l + m, IS_TILES[m % 3]
                    act.wait_ge(shared_up, i + 1)
                    if i >= 2:
                        act.wait_ge(shared_h, i - 1)
                    nc.scalar.activation(silu_s[i % 2][0:mw, :], bank(i % 2)[0:mw, :], ACT.Silu).then_inc(shared_silu, 1)
                for e in range(E + 3):
                    if e < E:
                        i = l * E + e
                        act.wait_ge(slotT_done, i + 1)
                        if i >= 2:
                            act.wait_ge(gu_done, i - 1)
                        nc.scalar.copy(slotsT[:, i % 2], bank(4 + i % 2)[:, 0:H].rearrange("p (k s) -> p k s", k=KT)
                                       ).then_inc(slotT_ready, 1)
                    if 0 < e <= E:
                        i = l * E + e - 1
                        act.wait_ge(gu_done, i + 1)
                        if i >= 2:
                            act.wait_ge(h_ready, i - 1)
                        nc.scalar.activation(silu_e[:, i % 2, :], bank(i % 2)[:, 0:I], ACT.Silu).then_inc(silu_done, 1)
                    if e >= 3:
                        i = l * E + e - 3
                        act.wait_ge(down_done, i + 1)
                        if i >= 4:
                            act.wait_ge(eo_stored[i % 4], 16 * (i // 4))
                        nc.scalar.copy(eo[(e - 3) % 4], bank(6 + i % 2)[:, 0:H]).then_inc(eo_ready, 1)

        @block.vector
        def _(dve):
            steps = [0]

            def settle(ins):
                steps[0] += 1
                ins.then_inc(dve_step, 1)
                dve.wait_ge(dve_step, steps[0])

            def norm(n):
                for t in range(NT):
                    if n == 0:
                        dve.wait_ge(x_loaded[t], 16)
                    last = nc.vector.bn_stats(stats[:, t, :], x_sb[:, t, :])
                settle(last)
                for t in range(NT):
                    last = nc.vector.bn_aggr(meanvar[:, t, :], stats[:, t, :])
                settle(last)
                nc.vector.tensor_scalar(vareps[:, :], meanvar[:, :, 1], EPS, None, ALU.add).then_inc(vareps_ready, 1)
                dve.wait_ge(rstd_ready, n + 1)
                for t in range(NT):
                    nc.vector.tensor_scalar(xn[:, t, :], x_sb[:, t, :], meanvar[:, t, 0:1], rstd[:, t:t + 1],
                                            ALU.subtract, ALU.mult).then_inc(xn_ready, 1)

            def pass1_units(l, g, units):
                for u in units:
                    j, t, _, width, on_diagonal = UNITS[u]
                    n = (l * NG + g) * NU + u
                    dve.wait_ge(s1_done, n + 1)
                    if n >= 2:
                        dve.wait_ge(s1_read, n - 1)
                    scores = bank(n % 2)[:, 0:width]
                    if on_diagonal:
                        nc.vector.tensor_tensor_reduce(
                            out=dump[:, n % 2, 0:width], in0=scores, in1=mask[:, HALF - width:HALF], scale=1.0, scalar=NEG,
                            op0=ALU.add, op1=ALU.max, accum_out=rowmax[:, j, t:t + 1]).then_inc(s1_read, 1)
                    else:
                        nc.vector.tensor_reduce(out=rowmax_a[:, j, t - NT // 2:t - NT // 2 + 1], in_=scores,
                                                axis=AX.X, op=ALU.max).then_inc(s1_read, 1)
                    if u == NU - 1:
                        dve.wait_ge(s1_read, n + 1)
                        nc.vector.tensor_tensor(rowmax[:, :, NT // 2:], rowmax[:, :, NT // 2:], rowmax_a[:, :, :],
                                                ALU.max).then_inc(max_ready, 1)

            def routing(l):
                cols = [P, NT, E]

                def wide(a):
                    return a.rearrange("p (t e) -> p t e", e=1).to_broadcast(cols)

                rev = revio[:, :, :].to_broadcast(cols)
                dve.wait_ge(logits_done, (l + 1) * NT)
                settle(nc.vector.tensor_copy(lg[:, :, :], bank(6)[:, 0:NT * E].rearrange("p (t e) -> p t e", t=NT)))
                settle(nc.vector.tensor_reduce(out=s8[:, 0, :], in_=lg[:, :, :], axis=AX.X, op=ALU.max))
                nc.vector.tensor_tensor(tmp[:, :, :], lg[:, :, :], wide(s8[:, 0, :]), ALU.subtract).then_inc(exp_in, 1)
                dve.wait_ge(exp_out, l + 1)
                settle(nc.vector.tensor_reduce(out=s8[:, 0, :], in_=ex[:, :, :], axis=AX.X, op=ALU.add))
                settle(nc.vector.reciprocal(s8[:, 1, :], s8[:, 0, :]))
                settle(nc.vector.tensor_tensor(sc[:, :, :], ex[:, :, :], wide(s8[:, 1, :]), ALU.mult))
                for k in range(TOPK):
                    settle(nc.vector.tensor_reduce(out=topw[:, k, :], in_=sc[:, :, :], axis=AX.X, op=ALU.max))
                    settle(nc.vector.tensor_tensor(tmp[:, :, :], sc[:, :, :], wide(topw[:, k, :]), ALU.is_equal))
                    settle(nc.vector.tensor_tensor(tmp[:, :, :], tmp[:, :, :], rev, ALU.mult))
                    settle(nc.vector.tensor_reduce(out=key[:, k, :], in_=tmp[:, :, :], axis=AX.X, op=ALU.max))
                    settle(nc.vector.tensor_tensor(hot[:, k], rev, wide(key[:, k, :]), ALU.is_equal))
                    if k == 0:
                        settle(nc.vector.scalar_tensor_tensor(out=sc[:, :, :], in0=hot[:, k], scalar=-4.0,
                                                              in1=sc[:, :, :], op0=ALU.mult, op1=ALU.add))
                nc.vector.tensor_tensor(hot_b[:, :, :], hot[:, 0], hot[:, 1], ALU.add).then_inc(hot_ready, 1)
                dve.wait_ge(rank_done, l + 1)
                ranks = bank(7)[:, 0:NT * E].rearrange("p (t e) -> p t e", t=NT)
                for k in range(TOPK):
                    settle(nc.vector.tensor_tensor(tmp[:, :, :], ranks, hot[:, k], ALU.mult))
                    settle(nc.vector.tensor_reduce(out=rank[:, k, :], in_=tmp[:, :, :], axis=AX.X, op=ALU.add))
                nc.vector.tensor_scalar(slot0[:, :, :], key[:, :, :], -float(CAP), float(E * CAP), ALU.mult, ALU.add)
                nc.vector.tensor_scalar(slot1[:, :, :], rank[:, :, :], float(CAP), float(4 * E * CAP), ALU.is_ge, ALU.mult)
                settle(nc.vector.tensor_scalar(slot2[:, :, :], rank[:, :, :], float(CAP - 1), None, ALU.min))
                nc.vector.tensor_tensor(get_at[:, :, :], slot0[:, :, :], slot2[:, :, :], ALU.add)
                settle(nc.vector.tensor_tensor(slot1[:, :, :], slot1[:, :, :], rank[:, :, :], ALU.add))
                nc.vector.tensor_tensor(put_at[:, :, :], slot0[:, :, :], slot1[:, :, :], ALU.add).then_inc(slots_known, 1)

            for l in range(LAYERS):
                norm(2 * l)
                if l == 0:
                    dve.wait_ge(rope_loaded, 16)
                for t in range(NT + 2):
                    if t < NT:
                        i = l * NT + t
                        dve.wait_ge(proj_done, i + 1)
                        if i >= 2:
                            dve.wait_ge(rope_sum, i - 1)
                        qk = bank(i % 2).rearrange("p (h b d) -> p h b d", h=2 * NH, b=2)
                        shape = [P, 2 * NH, 2, HH]

                        def table(m):
                            return rope_sb[:, l, t, m:m + 1, :].rearrange("p o (b d) -> p o b d", b=2).to_broadcast(shape)

                        nc.vector.tensor_tensor(rope_a[i % 2].rearrange("p (h b d) -> p h b d", h=2 * NH, b=2),
                                                qk, table(0), ALU.mult)
                        nc.vector.tensor_tensor(rope_b[i % 2].rearrange("p (h b d) -> p h b d", h=2 * NH, b=2),
                                                qk[:, :, ::-1, :], table(1), ALU.mult).then_inc(rope_mul, 1)
                    if 0 < t <= NT:
                        i = l * NT + t - 1
                        dve.wait_ge(part1_ready, i + 1)
                        r = roped[i % 2].rearrange("p (h d) -> p h d", h=2 * NH)
                        nc.vector.tensor_tensor(r, r, stacks[i % 2][:, :, 4, :], ALU.subtract).then_inc(rest_ready, 1)
                    if t > 1:
                        i = l * NT + t - 2
                        for c in range(3):
                            dve.wait_ge(stackT_done, 4 * i + c + 1)
                            dst = (q_st if c < 2 else k_st)[0:SR, 8 * (c % 2):8 * (c % 2) + 8, (t - 2) * P:(t - 1) * P]
                            nc.vector.tensor_copy(dst, bank(6 + c % 2)[0:SR, :].bitcast(BF16)
                                                  .rearrange("p (h s) -> p h s", h=8)).then_inc(stackT_read_v, 1)
                if l == 0:
                    dve.wait_ge(mask_ready, 1)
                pass1_units(l, 0, range(NU))
                for g in range(NG - 1):
                    for s in range(NS):
                        units = units_of(s)
                        if units and units[0] == 0:
                            dve.wait_ge(maxT_done, l * NG + g + 1)
                        pass1_units(l, g + 1, units)
                for t in range(NT):
                    i = l * NT + t
                    dve.wait_ge(oback_done, i + 1)
                    o4 = bank(i % 2).rearrange("p (h w) -> p h w", h=NH)
                    settle(nc.vector.reciprocal(recip[:, i % 2, :], o4[:, :, HD]))
                    if i >= 2:
                        dve.wait_ge(o2T_done, i - 1)
                    nc.vector.tensor_tensor(o_tok[:, i % 2, :].rearrange("p (h d) -> p h d", h=NH), o4[:, :, 0:HD],
                                            recip[:, i % 2, :].rearrange("p (h d) -> p h d", d=1)
                                            .to_broadcast([P, NH, HD]), ALU.mult).then_inc(o_ready, 1)
                    if t > 0:
                        dve.wait_ge(wo_done, i)
                        nc.vector.tensor_tensor(x_sb[:, t - 1, :], x_sb[:, t - 1, :], bank(4 + (i - 1) % 2)[:, 0:H],
                                                ALU.add).then_inc(attn_added, 1)
                dve.wait_ge(wo_done, (l + 1) * NT)
                nc.vector.tensor_tensor(x_sb[:, NT - 1, :], x_sb[:, NT - 1, :], bank(4 + (NT - 1) % 2)[:, 0:H],
                                        ALU.add).then_inc(attn_added, 1)
                dve.wait_ge(attn_added, (l + 1) * NT)
                norm(2 * l + 1)
                routing(l)
                for m in range(6):
                    i, (m0, mw) = 6 * l + m, IS_TILES[m % 3]
                    dve.wait_ge(shared_silu, i + 1)
                    nc.vector.tensor_tensor(hsT[0:mw, m % 3, (m // 3) * HALF:(m // 3 + 1) * HALF],
                                            silu_s[i % 2][0:mw, :], bank(2 + i % 2)[0:mw, :], ALU.mult).then_inc(shared_h, 1)
                for t in range(NT):
                    i = l * NT + t
                    dve.wait_ge(shared_down, i + 1)
                    nc.vector.tensor_tensor(x_sb[:, t, :], x_sb[:, t, :], bank(4 + i % 2)[:, 0:H],
                                            ALU.add).then_inc(shared_added, 1)
                for e in range(1, E + 2):
                    if e <= E:
                        i = l * E + e - 1
                        dve.wait_ge(silu_done, i + 1)
                        if i >= 2:
                            dve.wait_ge(hT_done, i - 1)
                        nc.vector.tensor_tensor(h_e[:, i % 2, :], silu_e[:, i % 2, :], bank(i % 2)[:, I:2 * I],
                                                ALU.mult).then_inc(h_ready, 1)
                    if e >= 2:
                        i = l * E + e - 2
                        dve.wait_ge(hT_done, i + 1)
                        if i >= 2:
                            dve.wait_ge(down_done, i - 1)
                        nc.vector.tensor_copy(hT_e[:, i % 2], bank(2 + i % 2)[0:IH, 0:2 * P]
                                              .rearrange("p (k s) -> p k s", k=2)).then_inc(hT_ready, 1)
                dve.wait_ge(shared_added, (l + 1) * NT)
                for k in range(TOPK):
                    for t in range(NT):
                        dve.wait_ge(got[t], 16 * TOPK * (l + 1))
                        last = nc.vector.scalar_tensor_tensor(out=x_sb[:, t, :], in0=gathered[:, k, t, :],
                                                              scalar=topw[:, k, t:t + 1], in1=x_sb[:, t, :],
                                                              op0=ALU.mult, op1=ALU.add)
                        if k == TOPK - 1:
                            last.then_inc(layer_done, 1)
                    if k == 0:
                        settle(last)
                dve.wait_ge(layer_done, (l + 1) * NT)

        @block.tensor
        def _(pe):
            def transposes_xn(n, t):
                i = n * NT + t
                pe.wait_ge(xn_ready, i + 1)
                if i >= 2:
                    pe.wait_ge(xnT_ready, i - 1)
                for k in range(KT):
                    last = nc.tensor.transpose(bank(4 + i % 2)[:, k * P:(k + 1) * P], xn[:, t, k * P:(k + 1) * P], ident[:, :])
                last.then_inc(xT_done, 1)

            def pass1(l, g, u):
                j, t, first, width, _ = UNITS[u]
                n = (l * NG + g) * NU + u
                if n >= 2:
                    pe.wait_ge(s1_read, n - 1)
                nc.tensor.matmul(bank(n % 2)[:, 0:width], q_st[0:SR, g * GH + j, t * P:(t + 1) * P],
                                 k_st[0:SR, g * GH + j, first:first + width], start=True, stop=True).then_inc(s1_done, 1)

            def transpose_max(l, g):
                n = l * NG + g
                pe.wait_ge(max_ready, n + 1)
                nc.tensor.transpose(bank(0)[0:GH * NT, 0:P], rowmax[:, :, :].rearrange("p h t -> p (h t)"),
                                    ident[:, :]).then_inc(maxT_done, 1)

            def pass2(l, g, s, pair):
                qc, kt = STEPS[s]
                first, width = columns(STEPS[s])
                u = 2 * ((l * NG + g) * NS + s) + pair
                if u >= 2:
                    pe.wait_ge(exp_done, u - 1)
                for j in range(2):
                    h = g * GH + 2 * pair + j
                    q0 = qc * HALF + first
                    last = nc.tensor.matmul(bank(2 + 2 * (u % 2) + j)[:, 0:width], k_st[0:SA, h, kt * P:(kt + 1) * P],
                                            q_st[0:SA, h, q0:q0 + width], start=True, stop=True)
                last.then_inc(s2_done, 1)

            def products_v(l, g, s):
                qc, kt = STEPS[s]
                first, width = columns(STEPS[s])
                n = (l * NG + g) * NS + s
                w = (l * NG + g) * NQ + qc
                starts, ends = kt == 0, s in STEP_ENDS
                if starts and w >= 2:
                    pe.wait_ge(oT_ready, w - 1)
                pe.wait_ge(exp_done, 2 * n + 2)
                if diagonal(STEPS[s]):
                    pe.wait_ge(masked, 2 * ((l * NG + g) * DIAGONALS + sum(diagonal(x) for x in STEPS[:s + 1])))
                for j in range(GH):
                    u = 2 * n + j // 2
                    last = nc.tensor.matmul(bank(6 + w % 2)[VW * j:VW * (j + 1), first:first + width],
                                            v_x[:, kt, g * GH + j, :], probs[u % 4][:, j % 2, 0:width],
                                            start=starts, stop=ends)
                last.then_inc(pv_done, 1)

            def back(l, t):
                i = l * NT + t
                if i >= 2:
                    pe.wait_ge(o_ready, i - 1)
                for g in range(NG):
                    last = nc.tensor.transpose(bank(i % 2)[:, g * P:(g + 1) * P], oT[:, g, t * P:(t + 1) * P], ident[:, :])
                last.then_inc(oback_done, 1)

            def o_transposes(l, t):
                i = l * NT + t
                pe.wait_ge(o_ready, i + 1)
                if i >= 2:
                    pe.wait_ge(o_T_ready, i - 1)
                for k in range(KT):
                    last = nc.tensor.transpose(bank(2 + i % 2)[:, k * P:(k + 1) * P], o_tok[:, i % 2, k * P:(k + 1) * P],
                                               ident[:, :])
                last.then_inc(o2T_done, 1)

            def o_product(l, t):
                i = l * NT + t
                pe.wait_ge(o_T_ready, i + 1)
                if i >= 2:
                    pe.wait_ge(attn_added, i - 1)
                for k in range(KT):
                    last = nc.tensor.matmul(bank(4 + i % 2)[:, 0:H], o_T[:, i % 2, k, :], wo_sb[:, l, k, :],
                                            start=(k == 0), stop=(k == KT - 1))
                last.then_inc(wo_done, 1)

            pe.wait_ge(consts_ready, 1)
            for l in range(LAYERS):
                if l > 0:
                    pe.wait_ge(eo_ready, l * E)
                pe.wait_ge(wqkv_loaded, 16 * (l + 1))
                for t in range(NT + 2):
                    if t < NT:
                        i = l * NT + t
                        if t == 0:
                            transposes_xn(2 * l, 0)
                        if t + 1 < NT:
                            transposes_xn(2 * l, t + 1)
                        pe.wait_ge(xnT_ready, 2 * l * NT + t + 1)
                        if i >= 2:
                            pe.wait_ge(rope_mul, i - 1)
                            pe.wait_ge(v_copied, i - 1)
                        for k in range(KT):
                            nc.tensor.matmul(bank(i % 2), xnT[:, k, t * P:(t + 1) * P], wqkv_sb[:, k, 0:2 * H],
                                             start=(k == 0), stop=(k == KT - 1))
                        for k in range(KT):
                            last = nc.tensor.matmul(bank(2 + i % 2)[:, 0:H], xnT[:, k, t * P:(t + 1) * P],
                                                    wqkv_sb[:, k, 2 * H:3 * H], start=(k == 0), stop=(k == KT - 1))
                        last.then_inc(proj_done, 1)
                    if t > 1:
                        i = l * NT + t - 2
                        pe.wait_ge(stack_ready, i + 1)
                        for c in range(4):
                            if c < 2:
                                if i > 0:
                                    if c == 0:
                                        pe.wait_ge(stackT_read_v, 3 * i)
                                    else:
                                        pe.wait_ge(stackT_read_a, i)
                            else:
                                pe.wait_ge(stackT_read_v, 3 * i + c - 1)
                            for h in range(8):
                                last = nc.tensor.transpose(
                                    bank(6 + c % 2)[0:SR, :].bitcast(BF16)[:, h * P:(h + 1) * P],
                                    stacks[i % 2][:, 8 * c + h, :, :].rearrange("p j d -> p (j d)"), ident_b[:, :])
                            last.then_inc(stackT_done, 1)
                pe.wait_ge(rope_mul, (l + 1) * NT)
                pe.wait_ge(v_copied, (l + 1) * NT)
                pe.wait_ge(xnT_ready, (2 * l + 1) * NT)
                pe.wait_ge(stackT_read_v, 3 * (l + 1) * NT)
                pe.wait_ge(stackT_read_a, (l + 1) * NT)
                for u in range(NU):
                    pass1(l, 0, u)
                transpose_max(l, 0)
                for g in range(NG):
                    pe.wait_ge(negmax_ready, l * NG + g + 1)
                    pe.wait_ge(shift_loaded, 16 * PARTS * (l * NG + g + 1))
                    for s in range(NS):
                        units = list(units_of(s)) if g + 1 < NG else []
                        if s == MAX_STEP and g + 1 < NG:
                            transpose_max(l, g + 1)
                        pass2(l, g, s, 0)
                        for u in units[:len(units) // 2]:
                            pass1(l, g + 1, u)
                        pass2(l, g, s, 1)
                        for u in units[len(units) // 2:]:
                            pass1(l, g + 1, u)
                        if s > 0:
                            products_v(l, g, s - 1)
                    products_v(l, g, NS - 1)
                if l == 0:
                    pe.wait_ge(wo_loaded, 16)
                pe.wait_ge(exp_done, 2 * (l + 1) * NG * NS)
                pe.wait_ge(oT_ready, (l + 1) * NG * NQ)
                for t in range(NT + 2):
                    if t < NT:
                        back(l, t)
                    if 0 < t <= NT:
                        o_transposes(l, t - 1)
                    if t > 1:
                        o_product(l, t - 2)
                if l == 0:
                    pe.wait_ge(moe_loaded, 64)
                pe.wait_ge(attn_added, (l + 1) * NT)
                for t in range(NT + 1):
                    if t < NT:
                        transposes_xn(2 * l + 1, t)
                    if t > 0:
                        pe.wait_ge(xnT_ready, (2 * l + 1) * NT + t)
                        for k in range(KT):
                            last = nc.tensor.matmul(bank(6)[:, (t - 1) * E:t * E], xnT[:, k, (t - 1) * P:t * P],
                                                    gate_sb[:, k, :], start=(k == 0), stop=(k == KT - 1))
                        last.then_inc(logits_done, 1)

                def shared_product(m):
                    i, (m0, mw) = 6 * l + m, IS_TILES[m % 3]
                    if i >= 2:
                        pe.wait_ge(shared_h, i - 1)
                    for b, off in ((0, 0), (2, IS)):
                        for k in range(KT):
                            last = nc.tensor.matmul(bank(b + i % 2)[0:mw, :], wsgu_sb[:, k, off + m0:off + m0 + mw],
                                                    xnT[:, k, (m // 3) * HALF:(m // 3 + 1) * HALF],
                                                    start=(k == 0), stop=(k == KT - 1))
                    last.then_inc(shared_up, 1)

                shared_product(0)
                shared_product(1)
                pe.wait_ge(hot_ready, l + 1)
                nc.tensor.matmul(bank(7)[:, 0:NT * E], before[:, :], hot_b[:, :, :].rearrange("p t e -> p (t e)"),
                                 start=True, stop=False)
                for j in range(NT - 1):
                    last = nc.tensor.matmul(bank(7)[:, (j + 1) * E:NT * E].rearrange("p (t e) -> p t e", e=E),
                                            ones_b[:, :], hot_b[:, j:j + 1, :].to_broadcast([P, NT - 1 - j, E]),
                                            start=False, stop=(j == NT - 2))
                last.then_inc(rank_done, 1)
                for m in range(2, 6):
                    shared_product(m)
                for t in range(NT):
                    i = l * NT + t
                    if t == 0:
                        pe.wait_ge(shared_h, 6 * (l + 1))
                        pe.wait_ge(xnT_ready, (2 * l + 2) * NT)
                    if i >= 2:
                        pe.wait_ge(shared_added, i - 1)
                    for m, (m0, mw) in enumerate(IS_TILES):
                        last = nc.tensor.matmul(bank(4 + i % 2)[:, 0:H], hsT[0:mw, m, t * P:(t + 1) * P], wsd_sb[0:mw, m, :],
                                                start=(m == 0), stop=(m == 2))
                    last.then_inc(shared_down, 1)
                pe.wait_ge(shared_added, (l + 1) * NT)
                pe.wait_ge(slots_known, l + 1)
                for e in range(E + 3):
                    if e < E:
                        i = l * E + e
                        if e % 4 == 0:
                            pe.wait_ge(slots_loaded[e // 4], 16 * (l + 1))
                        if i >= 2:
                            pe.wait_ge(slotT_ready, i - 1)
                        for k in range(KT):
                            last = nc.tensor.transpose(bank(4 + i % 2)[:, k * P:(k + 1) * P], slots[:, e, k * P:(k + 1) * P],
                                                       ident[:, :])
                        last.then_inc(slotT_done, 1)
                    if 0 < e <= E:
                        i = l * E + e - 1
                        pe.wait_ge(slotT_ready, i + 1)
                        pe.wait_ge(expert_loaded[e - 1], 32 * (l + 1))
                        if i >= 2:
                            pe.wait_ge(h_ready, i - 1)
                        for k in range(KT):
                            last = nc.tensor.matmul(bank(i % 2)[:, 0:2 * I], slotsT[:, i % 2, k, :], wgu_sb[:, e - 1, k, :],
                                                    start=(k == 0), stop=(k == KT - 1))
                        last.then_inc(gu_done, 1)
                    if 1 < e <= E + 1:
                        i = l * E + e - 2
                        pe.wait_ge(h_ready, i + 1)
                        if i >= 2:
                            pe.wait_ge(hT_ready, i - 1)
                        for k in range(2):
                            last = nc.tensor.transpose(bank(2 + i % 2)[0:IH, k * P:(k + 1) * P],
                                                       h_e[:, i % 2, k * IH:(k + 1) * IH], ident[:, :])
                        last.then_inc(hT_done, 1)
                    if e > 2:
                        i = l * E + e - 3
                        pe.wait_ge(hT_ready, i + 1)
                        if i >= 2:
                            pe.wait_ge(eo_ready, i - 1)
                        for k in range(2):
                            last = nc.tensor.matmul(bank(6 + i % 2)[:, 0:H], hT_e[:, i % 2, k, :], wd_sb[:, e - 3, k, :],
                                                    start=(k == 0), stop=(k == 1))
                        last.then_inc(down_done, 1)


def rope_tables():
    inv_freq = (1.0 / 10000.0 ** (np.arange(0, HD, 2, dtype=np.float32) / HD)).astype(np.float32)
    freqs = np.einsum("i,j->ij", np.arange(S, dtype=np.float32), inv_freq)
    cos, sin = np.cos(freqs).astype(np.float32), np.sin(freqs).astype(np.float32)
    rows = []
    for a, b in ((cos, sin), (sin, cos)):
        rows.append(np.stack([np.concatenate([a, a], 1), np.concatenate([-b, b], 1)], 1))
    table = np.stack(rows)
    return np.ascontiguousarray(table.reshape(LAYERS, NT, P, 2, HD).transpose(2, 0, 1, 3, 4))


def kernel(**inputs):
    import numpy as _np
    import concourse.bacc as _bacc
    from concourse import mybir as _mybir
    from concourse.bass_utils import run_bass_kernel_spmd as _run

    a = {k: _np.asarray(v) for k, v in inputs.items()}

    def qkv(which):
        return _np.concatenate([a[f"L0_attn_{which}_W{m}"].T for m in "qkv"], axis=1)

    arrays = {
        "x": a["L0_attn_a_hidden_states"].reshape(S, H),
        "wqkv": _np.stack([qkv("a"), qkv("b")]),
        "wo": _np.stack([a["L0_attn_a_Wo"].T, a["L0_attn_b_Wo"].T]),
        "gate": a["L0_ffn_gate_w"].T,
        "wgu": _np.concatenate([a["L0_ffn_w_gate"], a["L0_ffn_w_up"]], axis=2),
        "wdown": a["L0_ffn_w_down"],
        "wsgu": _np.concatenate([a["L0_ffn_ws_gate"], a["L0_ffn_ws_up"]], axis=1),
        "wsdown": a["L0_ffn_ws_down"],
        "rope": rope_tables(),
    }
    nc = _bacc.Bacc("TRN2", target_bir_lowering=False, num_devices=1)
    feeds, args = {}, []
    for name, value in arrays.items():
        feeds[f"{name}_dram"] = _np.ascontiguousarray(value)
        args.append(nc.dram_tensor(f"{name}_dram", value.shape, _mybir.dt.from_np(value.dtype), kind="ExternalInput").ap())
    args.append(nc.dram_tensor("out_dram", (S, H), _mybir.dt.float32, kind="ExternalOutput").ap())
    build(nc, *args)
    r = _run(nc, [feeds], core_ids=[0])
    return r.results[0]["out_dram"].reshape(1, S, H)
```

```python
import numpy as np
from contextlib import ExitStack

import concourse.bass as bass
from concourse import mybir

F32 = mybir.dt.float32
BF16 = mybir.dt.bfloat16
U32 = mybir.dt.uint32
ALU = mybir.AluOpType
ACT = mybir.ActivationFunctionType
AX = mybir.AxisListType

P = 128
S = 1024
NT = S // P
H = 256
KT = H // P
NH = 16
HD = H // NH
HH = HD // 2
LAYERS = 2
GH = 4
NG = NH // GH
PARTS = 3
NB = 6
SR = NB * HD
SA = SR + PARTS
VW = 32
HALF = 512
NQ = S // HALF
E = 16
CAP = 128
TOPK = 2
I = 176
IH = I // 2
IS = 352
IS_TILES = [(0, 128), (128, 128), (256, 96)]
EPS = 1e-5
NEG = -3.0e38
EXPERT_WORDS = KT * 2 * I + 2 * H
GROUP_WORDS = GH * S
FREED = [min(E, (g + 1) * GROUP_WORDS // EXPERT_WORDS) for g in range(NG - 1)] + [E]

STEPS = [(0, 0), (0, 1), (0, 2), (0, 3), (1, 0), (1, 4), (1, 5), (1, 6), (1, 7), (1, 1), (1, 2), (1, 3)]
NS = len(STEPS)
STEP_ENDS = {3: 0, 11: 1}
NARROW = [[] for _ in range(NT)]
WIDE = []
for t in range(NT):
    keys = (t + 1) * P
    for j in range(GH):
        if keys > HALF:
            NARROW[t].append((j, t, 0, HALF, False))
            NARROW[t].append((j, t, HALF, keys - HALF, True))
        else:
            NARROW[t].append((j, t, 0, keys, True))
        WIDE.append((j, t, 0, keys, True))
NARROWS, WIDES = sum(map(len, NARROW)), len(WIDE)
UNITS = NARROWS + (NG - 1) * WIDES
MAX_STEP = 9


def diagonal(step):
    qc, kt = step
    return kt * P >= qc * HALF


DIAGONALS = sum(diagonal(s) for s in STEPS)


def columns(step):
    qc, kt = step
    first = max(kt * P - qc * HALF, 0)
    return first, HALF - first


def wide_units(s):
    work = np.cumsum([0] + [columns(x)[1] for x in STEPS[:MAX_STEP]]) / sum(columns(x)[1] for x in STEPS[:MAX_STEP])
    keys = np.cumsum([u[3] + P for u in WIDE])
    done = [int(np.searchsorted(keys, w * keys[-1] + 0.5)) for w in work]
    return range(done[s], done[s + 1]) if s < MAX_STEP else range(0)


def build(nc, x, wqkv, wo, gate, wgu, wdown, wsgu, wsdown, rope, out):
    ctx = ExitStack()
    with ctx:
        def sb(name, shape, dt=F32):
            return ctx.enter_context(nc.sbuf_tensor(name, shape, dt))

        def sem(name):
            return ctx.enter_context(nc.semaphore(name))

        x_sb = sb("x_sb", [P, NT, H])
        norms = sb("norms", [P, 2 * NT * H])
        xn = norms[:, 0:NT * H].rearrange("p (t d) -> p t d", t=NT)
        xnT = norms[:, NT * H:2 * NT * H].rearrange("p (k s) -> p k s", k=KT)
        oT = norms[:, :].rearrange("p (g s) -> p g s", g=NG)
        QKW, VWORDS = NG * GROUP_WORDS, NT * NH * VW
        arena = sb("arena", [P, QKW + VWORDS])
        qk_st = arena[:, 0:QKW].bitcast(BF16).rearrange("p (g b h s) -> p g b h s", g=NG, b=2, h=GH)
        v_x = arena[:, QKW:].rearrange("p (t h w) -> p t h w", t=NT, h=NH)
        GUW = KT * 2 * I
        experts = arena[:, 0:E * EXPERT_WORDS].rearrange("p (e w) -> p e w", e=E)
        wgu_sb = experts[:, :, 0:GUW].rearrange("p e (k n) -> p e k n", k=KT)
        wd_sb = experts[0:IH, :, GUW:EXPERT_WORDS].rearrange("p e (k n) -> p e k n", k=2)
        stage = sb("stage", [P, 7 * 2 * H])
        rope_a = [stage[:, 1024 * b:1024 * b + 512] for b in range(2)]
        rope_b = [stage[:, 1024 * b + 512:1024 * b + 1024] for b in range(2)]
        roped = [stage[:, 2048 + 512 * b:2560 + 512 * b] for b in range(3)]
        silu_s = [stage[:, 512 * b:512 * b + 512] for b in range(2)]
        eo = [stage[:, 1024 + 256 * b:1280 + 256 * b] for b in range(4)]
        parts_all = sb("parts_all", [P, 3 * NH * NB * HD])
        parts = parts_all[:, :].bitcast(BF16).rearrange("p (b h j d) -> p b h j d", b=3, h=2 * NH, j=NB)
        hsT = parts_all[:, 0:3 * S].rearrange("p (m s) -> p m s", m=3)
        probs_all = sb("probs", [P, 8, HALF])
        slots = probs_all[:, :, :].rearrange("p a (b d) -> p (a b) d", d=H)
        gathered = slots.rearrange("p (k t) d -> p k t d", k=TOPK)
        wqkv_sb = sb("wqkv_sb", [P, KT, 3 * H])
        wo_sb = sb("wo_sb", [P, LAYERS, KT, H])
        gate_sb = sb("gate_sb", [P, KT, E])
        wsgu_sb = sb("wsgu_sb", [P, KT, 2 * IS])
        wsd_sb = sb("wsd_sb", [P, 3, H])
        rope_sb = sb("rope_sb", [P, LAYERS, NT, 2, HD])
        ident = sb("ident", [P, P])
        ident_b = sb("ident_b", [P, P], BF16)
        before = sb("before", [P, P], BF16)
        ones_b = sb("ones_b", [P, P], BF16)
        mask = sb("mask", [P, S], BF16)
        revio = sb("revio", [P, 1, E])
        revio_i = sb("revio_i", [P, E], mybir.dt.int32)
        neghalf = sb("neghalf", [P, NT])
        stats = sb("stats", [P, NT, 6])
        meanvar = sb("meanvar", [P, NT, 2])
        vareps = sb("vareps", [P, NT])
        rstd = sb("rstd", [P, NT])
        dump = sb("dump", [P, 2, S], BF16)
        rowmax = sb("rowmax", [P, GH, NT])
        rowmax_a = sb("rowmax_a", [P, GH, NT // 2])
        negmax = sb("negmax", [GH * NT, P])
        negrest = sb("negrest", [GH * NT, P])
        shift = sb("shift", [GH * NT, PARTS, P], BF16)
        recip = sb("recip", [P, 2, NH])
        o_tok = sb("o_tok", [P, 2, H])
        o_T = sb("o_T", [P, 2, KT, P])
        slotsT = sb("slotsT", [P, 2, KT, P])
        silu_e = sb("silu_e", [P, 2, I])
        h_e = sb("h_e", [P, 2, I])
        hT_e = sb("hT_e", [IH, 2, 2, P])
        lg = sb("lg", [P, NT, E])
        ex = sb("ex", [P, NT, E])
        sc = sb("sc", [P, NT, E])
        tmp = sb("tmp", [P, NT, E])
        hot = sb("hot", [P, TOPK, NT, E])
        hot_b = sb("hot_b", [P, NT, E], BF16)
        s8 = sb("s8", [P, 2, NT])
        topw = sb("topw", [P, TOPK, NT])
        key = sb("key", [P, TOPK, NT])
        rank = sb("rank", [P, TOPK, NT])
        slot0 = sb("slot0", [P, TOPK, NT])
        slot1 = sb("slot1", [P, TOPK, NT])
        slot2 = sb("slot2", [P, TOPK, NT])
        put_at = sb("put_at", [P, TOPK, NT], U32)
        get_at = sb("get_at", [P, TOPK, NT], U32)
        zeros = o_tok[:, :, :]

        slots_dram = nc.dram_tensor("slots_dram", (E * CAP, H), F32, kind="Internal").ap()
        eo_dram = nc.dram_tensor("eo_dram", (E * CAP, H), F32, kind="Internal").ap()

        banks = ctx.enter_context(nc.psum_tensor("banks", [P, 8, HALF], F32))

        def bank(n):
            return banks[:, n, :]


        def heads(b, h):
            return qk_st[:, h // GH, b, h % GH, :]

        def chunk(c, t):
            return qk_st[0:SR, 2 * (c % 2):2 * (c % 2) + 2, c // 2, :, t * P:(t + 1) * P]

        def chunk_bank(c):
            return bank(6 + c % 2)[0:SR, :].bitcast(BF16).rearrange("p (g h s) -> p g h s", g=2, h=GH)

        def narrow_index(l, t):
            return l * UNITS + sum(len(x) for x in NARROW[:t])

        def wide_index(l, g):
            return l * UNITS + NARROWS + (g - 1) * WIDES

        x_loaded = [sem(f"x_loaded{t}") for t in range(NT)]
        wqkv_loaded = sem("wqkv_loaded")
        wo_loaded = sem("wo_loaded")
        rope_loaded = sem("rope_loaded")
        moe_loaded = sem("moe_loaded")
        consts_ready = sem("consts_ready")
        mask_ready = sem("mask_ready")
        zeros_ready = sem("zeros_ready")
        slots_zeroed = sem("slots_zeroed")
        moments_ready = sem("moments_ready")
        ones_loaded = sem("ones_loaded")
        rstd_ready = sem("rstd_ready")
        xn_ready = sem("xn_ready")
        xT_done = sem("xT_done")
        xnT_ready = sem("xnT_ready")
        proj_done = sem("proj_done")
        rope_mul = sem("rope_mul")
        rope_sum = sem("rope_sum")
        part1_ready = sem("part1_ready")
        rest_ready = sem("rest_ready")
        part2_ready = sem("part2_ready")
        parts_ready = sem("parts_ready")
        stackT_done = sem("stackT_done")
        stackT_read_v = sem("stackT_read_v")
        stackT_read_a = sem("stackT_read_a")
        v_copied = sem("v_copied")
        v_fixed = sem("v_fixed")
        s1_done = sem("s1_done")
        s1_read = sem("s1_read")
        max_ready = sem("max_ready")
        maxT_done = sem("maxT_done")
        negmax_ready = sem("negmax_ready")
        shift_ready = sem("shift_ready")
        shift_loaded = sem("shift_loaded")
        s2_done = sem("s2_done")
        exp_done = sem("exp_done")
        masked = sem("masked")
        pv_done = sem("pv_done")
        oT_ready = sem("oT_ready")
        oback_done = sem("oback_done")
        o_ready = sem("o_ready")
        o2T_done = sem("o2T_done")
        o_T_ready = sem("o_T_ready")
        wo_done = sem("wo_done")
        attn_added = sem("attn_added")
        logits_done = sem("logits_done")
        logits_read = sem("logits_read")
        exp_in = sem("exp_in")
        exp_out = sem("exp_out")
        hot_ready = sem("hot_ready")
        rank_done = sem("rank_done")
        rank_read = sem("rank_read")
        slots_known = sem("slots_known")
        scattered = sem("scattered")
        slots_loaded = [sem(f"slots_loaded{n}") for n in range(4)]
        shared_up = sem("shared_up")
        shared_silu = sem("shared_silu")
        shared_h = sem("shared_h")
        shared_down = sem("shared_down")
        shared_added = sem("shared_added")
        expert_loaded = [sem(f"expert_loaded{e}") for e in range(E)]
        slotT_done = sem("slotT_done")
        slotT_ready = sem("slotT_ready")
        gu_done = sem("gu_done")
        silu_done = sem("silu_done")
        h_ready = sem("h_ready")
        hT_done = sem("hT_done")
        hT_ready = sem("hT_ready")
        down_done = sem("down_done")
        eo_ready = sem("eo_ready")
        eo_stored = [sem(f"eo_stored{n}") for n in range(4)]
        got = [sem(f"got{t}") for t in range(NT)]
        layer_done = sem("layer_done")
        out_stored = sem("out_stored")
        dve_step = sem("dve_step")
        pool_step = sem("pool_step")

        block = ctx.enter_context(nc.Block())

        @block.sync
        def _(sp):
            for t in range(NT):
                sp.dma_start(x_sb[:, t, :], x[t * P:(t + 1) * P, :]).then_inc(x_loaded[t], 16)
            sp.dma_start(wqkv_sb[:, :, :], wqkv[0].rearrange("(k p) n -> p k n", p=P)).then_inc(wqkv_loaded, 16)
            sp.dma_start(rope_sb[:, :, :, :, :], rope.rearrange("p l t m d -> p l t m d")).then_inc(rope_loaded, 16)
            sp.dma_start(wo_sb[:, :, :, :], wo.rearrange("l (k p) n -> p l k n", p=P)).then_inc(wo_loaded, 16)
            sp.dma_start(gate_sb[:, :, :], gate.rearrange("(k p) e -> p k e", p=P)).then_inc(moe_loaded, 16)
            sp.dma_start(wsgu_sb[:, :, :], wsgu.rearrange("(k p) n -> p k n", p=P)).then_inc(moe_loaded, 16)
            sp.dma_start(wsd_sb[:, 0:2, :], wsdown[0:2 * P, :].rearrange("(k p) n -> p k n", p=P)).then_inc(moe_loaded, 16)
            sp.dma_start(wsd_sb[0:IS - 2 * P, 2, :], wsdown[2 * P:IS, :]).then_inc(moe_loaded, 16)
            sp.wait_ge(zeros_ready, 1)
            for n in range(8):
                sp.dma_start(slots_dram[n * 2 * P:(n + 1) * 2 * P, :].rearrange("(k p) d -> p k d", p=P),
                             zeros).then_inc(slots_zeroed, 16)

            def load_experts(l, g):
                sp.wait_ge(pv_done, (l * NG + g + 1) * NS)
                for e in range(FREED[g - 1] if g else 0, FREED[g]):
                    sp.dma_start(wgu_sb[:, e, :, :], wgu[e].rearrange("(k p) n -> p k n", p=P)).then_inc(expert_loaded[e], 16)
                    sp.dma_start(wd_sb[:, e, :, :], wdown[e].rearrange("(k p) n -> p k n", p=IH)).then_inc(expert_loaded[e], 16)

            for l in range(LAYERS):
                if l == 0:
                    sp.wait_ge(consts_ready, 1)
                else:
                    sp.wait_ge(down_done, l * E)
                for g in range(NG):
                    for part in range(PARTS):
                        sp.dma_start(qk_st[SR + part:SR + part + 1, g, 1], ones_b[0:GH * NT, :]).then_inc(ones_loaded, 16)
                for g in range(NG):
                    sp.wait_ge(shift_ready, l * NG + g + 1)
                    for part in range(PARTS):
                        sp.dma_start(qk_st[SR + part:SR + part + 1, g, 0], shift[:, part, :]).then_inc(shift_loaded, 16)
                    if g > 0:
                        load_experts(l, g - 1)
                load_experts(l, NG - 1)
                if l + 1 < LAYERS:
                    sp.wait_ge(proj_done, NT * (l + 1))
                    sp.dma_start(wqkv_sb[:, :, :], wqkv[l + 1].rearrange("(k p) n -> p k n", p=P)).then_inc(wqkv_loaded, 16)
                sp.wait_ge(scattered, (l + 1) * TOPK * NT * 16)
                for n in range(4):
                    sp.dma_start(slots[:, 4 * n:4 * n + 4, :],
                                 slots_dram[n * 4 * P:(n + 1) * 4 * P, :].rearrange("(e p) d -> p e d", p=P)
                                 ).then_inc(slots_loaded[n], 16)
                for e in range(E):
                    sp.wait_ge(eo_ready, l * E + e + 1)
                    sp.dma_start(eo_dram[e * CAP:(e + 1) * CAP, :], eo[e % 4]).then_inc(eo_stored[e % 4], 16)
            for t in range(NT):
                sp.wait_ge(layer_done, (LAYERS - 1) * NT + t + 1)
                sp.dma_start(out[t * P:(t + 1) * P, :], x_sb[:, t, :]).then_inc(out_stored, 16)
            sp.wait_ge(out_stored, 16 * NT)

        @block.gpsimd
        def _(pool):
            steps = [0]

            def settle(ins):
                steps[0] += 1
                ins.then_inc(pool_step, 1)
                pool.wait_ge(pool_step, steps[0])

            nc.gpsimd.memset(neghalf[:, :], -0.5)
            nc.gpsimd.memset(zeros, 0.0).then_inc(zeros_ready, 1)
            nc.gpsimd.memset(ident[:, :], 0.0)
            nc.gpsimd.memset(before[:, :], 1.0)
            nc.gpsimd.memset(ones_b[:, :], 1.0)
            nc.gpsimd.iota(revio_i[:, :], pattern=[[-1, E]], base=E, channel_multiplier=0)
            settle(nc.gpsimd.memset(mask[:, :], 0.0))
            nc.gpsimd.tensor_copy(revio[:, 0, :], revio_i[:, :])
            settle(nc.gpsimd.affine_select(out=ident[:, :], in_=ident[:, :], compare_op=ALU.not_equal, fill=1.0,
                                           base=0, pattern=[[-1, P]], channel_multiplier=1))
            nc.gpsimd.tensor_copy(ident_b[:, :], ident[:, :])
            nc.gpsimd.affine_select(out=before[:, :], in_=before[:, :], compare_op=ALU.is_gt, fill=0.0,
                                    base=0, pattern=[[1, P]], channel_multiplier=-1).then_inc(consts_ready, 1)
            nc.gpsimd.affine_select(out=mask[:, S - P:S], in_=mask[:, S - P:S],
                                    compare_op=ALU.is_ge, fill=NEG, base=0, pattern=[[-1, P]],
                                    channel_multiplier=1).then_inc(mask_ready, 1)

            def deviation(n, t):
                i = n * NT + t
                pool.wait_ge(moments_ready, i + 1)
                settle(nc.gpsimd.tensor_scalar(vareps[:, t:t + 1], meanvar[:, t, 1:2], EPS, None, ALU.add))
                nc.gpsimd.tensor_tensor(rstd[:, t:t + 1], vareps[:, t:t + 1], neghalf[:, 0:1], ALU.pow).then_inc(rstd_ready, 1)

            def causal(l, g, s):
                n = (l * NG + g) * NS + s
                if diagonal(STEPS[s]):
                    for pair in range(2):
                        pool.wait_ge(exp_done, 4 * n + 2 * pair + 2)
                        b = (4 * n + 2 * pair) % 8
                        blocks = probs_all[:, b:b + 2, 0:P]
                        nc.gpsimd.affine_select(out=blocks, in_=blocks, compare_op=ALU.is_ge, fill=0.0, base=0,
                                                pattern=[[0, 2], [1, P]], channel_multiplier=-1).then_inc(masked, 1)

            def split_max(l, g):
                n = l * NG + g
                pool.wait_ge(negmax_ready, n + 1)
                if n:
                    pool.wait_ge(shift_loaded, 16 * PARTS * n)
                settle(nc.gpsimd.tensor_copy(shift[:, 0, :], negmax[:, :]))
                settle(nc.gpsimd.tensor_tensor(negrest[:, :], negmax[:, :], shift[:, 0, :], ALU.subtract))
                settle(nc.gpsimd.tensor_copy(shift[:, 1, :], negrest[:, :]))
                nc.gpsimd.tensor_tensor(shift[:, 2, :], negrest[:, :], shift[:, 1, :], ALU.subtract).then_inc(shift_ready, 1)

            def gather(l, t):
                for k in range(TOPK):
                    nc.gpsimd.indirect_dma_start(
                        out=gathered[:, k, t, :], out_offset=None, in_=eo_dram,
                        in_offset=bass.IndirectOffsetOnAxis(ap=get_at[:, k, t:t + 1], axis=0)
                    ).then_inc(got[t], 16)

            for l in range(LAYERS):
                if l > 0:
                    for t in range(4):
                        gather(l - 1, t)
                for t in range(2):
                    deviation(2 * l, t)
                for t in range(NT + 1):
                    if l > 0 and t + 4 < NT:
                        gather(l - 1, t + 4)
                    if t + 2 < NT:
                        deviation(2 * l, t + 2)
                    if t < NT:
                        i = l * NT + t
                        pool.wait_ge(rope_mul, i + 1)
                        if i >= 3:
                            pool.wait_ge(parts_ready, i - 2)
                        nc.gpsimd.tensor_tensor(roped[i % 3], rope_a[i % 2], rope_b[i % 2], ALU.add).then_inc(rope_sum, 1)
                    if t > 0:
                        i = l * NT + t - 1
                        pool.wait_ge(part2_ready, i + 1)
                        rest, to = roped[i % 3].rearrange("p (h d) -> p h d", d=HD), parts[:, i % 3]
                        nc.gpsimd.tensor_tensor(to[:, 0:NH, 5, :], rest[:, 0:NH], to[:, 0:NH, 1, :], ALU.subtract)
                        nc.gpsimd.tensor_tensor(to[:, NH:, 2, :], rest[:, NH:], to[:, NH:, 1, :],
                                                ALU.subtract).then_inc(parts_ready, 1)
                nc.gpsimd.memset(v_x[:, :, :, HD + 1:VW], 0.0)
                nc.gpsimd.memset(v_x[:, :, :, HD:HD + 1], 1.0).then_inc(v_fixed, 1)
                pool.wait_ge(v_fixed, l + 1)
                split_max(l, 0)
                for g in range(NG):
                    for s in range(NS):
                        if s == MAX_STEP and g + 1 < NG:
                            split_max(l, g + 1)
                        causal(l, g, s)
                for t in range(NT):
                    deviation(2 * l + 1, t)
                pool.wait_ge(slots_known, l + 1)
                if l == 0:
                    pool.wait_ge(slots_zeroed, 16 * 8)
                else:
                    for n in range(4):
                        pool.wait_ge(slots_loaded[n], 16 * l)
                for t in range(NT):
                    for k in range(TOPK):
                        nc.gpsimd.indirect_dma_start(
                            out=slots_dram, out_offset=bass.IndirectOffsetOnAxis(ap=put_at[:, k, t:t + 1], axis=0),
                            in_=xn[:, t, :], in_offset=None, bounds_check=E * CAP - 1, oob_is_err=False
                        ).then_inc(scattered, 16)
                for n in range(4):
                    pool.wait_ge(eo_stored[n], 16 * (l + 1) * E // 4)
            for t in range(NT):
                gather(LAYERS - 1, t)

        @block.scalar
        def _(act):
            def copy_xT(n, t, b):
                act.wait_ge(xT_done, n * NT + t + 1)
                nc.scalar.copy(xnT[:, :, t * P:(t + 1) * P],
                               bank(b)[:, 0:H].rearrange("p (k s) -> p k s", k=KT)).then_inc(xnT_ready, 1)

            def exps(l, g, s):
                n = (l * NG + g) * NS + s
                first, width = columns(STEPS[s])
                if n >= 2:
                    act.wait_ge(pv_done, n - 1)
                for j in range(GH):
                    u = 4 * n + j
                    act.wait_ge(s2_done, u + 1)
                    nc.scalar.activation(probs_all[:, u % 8, 0:width], bank(4 + u % 3)[:, 0:width],
                                         ACT.Exp, scale=HD ** -0.5).then_inc(exp_done, 1)

            def copy_oT(l, g, qc):
                end = [s for s in STEP_ENDS if STEP_ENDS[s] == qc][0]
                act.wait_ge(pv_done, (l * NG + g) * NS + end + 1)
                nc.scalar.copy(oT[:, g, qc * HALF:(qc + 1) * HALF], bank(7)).then_inc(oT_ready, 1)

            def negate_max(l, g):
                n = l * NG + g
                act.wait_ge(maxT_done, n + 1)
                if n:
                    act.wait_ge(shift_ready, n)
                nc.scalar.mul(negmax[:, :], bank(0)[0:GH * NT, 0:P], -1.0).then_inc(negmax_ready, 1)

            for l in range(LAYERS):
                copy_xT(2 * l, 0, 5)
                for t in range(NT + 2):
                    if t + 1 < NT:
                        copy_xT(2 * l, t + 1, 5)
                    if t < NT:
                        i = l * NT + t
                        act.wait_ge(proj_done, i + 1)
                        nc.scalar.copy(v_x[:, t, :, 0:HD], bank(4)[:, 0:H].rearrange("p (h d) -> p h d", h=NH)
                                       ).then_inc(v_copied, 1)
                        act.wait_ge(rope_sum, i + 1)
                        if i >= 3:
                            act.wait_ge(stackT_done, 4 * (i - 2))
                        whole, to = roped[i % 3].rearrange("p (h j d) -> p h j d", j=1, d=HD), parts[:, i % 3]
                        nc.scalar.copy(to[:, 0:NH, 0:5:2, :], whole[:, 0:NH].to_broadcast([P, NH, 3, HD]))
                        nc.scalar.copy(to[:, NH:, 3:6, :], whole[:, NH:].to_broadcast([P, NH, 3, HD])).then_inc(part1_ready, 1)
                    if 0 < t <= NT:
                        i = l * NT + t - 1
                        act.wait_ge(rest_ready, i + 1)
                        rest, to = roped[i % 3].rearrange("p (h j d) -> p h j d", j=1, d=HD), parts[:, i % 3]
                        nc.scalar.copy(to[:, 0:NH, 1:4:2, :], rest[:, 0:NH].to_broadcast([P, NH, 2, HD]))
                        nc.scalar.copy(to[:, NH:, 0:2, :], rest[:, NH:].to_broadcast([P, NH, 2, HD])).then_inc(part2_ready, 1)
                    if t > 1:
                        i = l * NT + t - 2
                        for c in (1, 3):
                            act.wait_ge(stackT_done, 4 * i + c + 1)
                            nc.scalar.copy(chunk(c, t - 2), chunk_bank(c)).then_inc(stackT_read_a, 1)
                negate_max(l, 0)
                for g in range(NG):
                    for s in range(NS):
                        if s == MAX_STEP and g + 1 < NG:
                            negate_max(l, g + 1)
                        exps(l, g, s)
                        if s - 1 in STEP_ENDS:
                            copy_oT(l, g, STEP_ENDS[s - 1])
                        if s == 0 and g > 0:
                            copy_oT(l, g - 1, 1)
                copy_oT(l, NG - 1, 1)
                for t in range(NT + 5):
                    if 0 < t <= NT:
                        i = l * NT + t - 1
                        act.wait_ge(o2T_done, i + 1)
                        if i >= 2:
                            act.wait_ge(wo_done, i - 1)
                        nc.scalar.copy(o_T[:, i % 2], bank(2)[:, 0:H].rearrange("p (k s) -> p k s", k=KT)
                                       ).then_inc(o_T_ready, 1)
                    if t >= 5:
                        copy_xT(2 * l + 1, t - 5, 6 + (t - 5) % 2)
                act.wait_ge(exp_in, l + 1)
                nc.scalar.activation(ex[:, :, :], tmp[:, :, :], ACT.Exp).then_inc(exp_out, 1)
                for m in range(6):
                    i, (_, mw) = 6 * l + m, IS_TILES[m % 3]
                    act.wait_ge(shared_up, i + 1)
                    if i >= 2:
                        act.wait_ge(shared_h, i - 1)
                    nc.scalar.activation(silu_s[i % 2][0:mw, :], bank(i % 2)[0:mw, :], ACT.Silu).then_inc(shared_silu, 1)
                for e in range(E + 3):
                    if e < E:
                        i = l * E + e
                        act.wait_ge(slotT_done, i + 1)
                        if i >= 2:
                            act.wait_ge(gu_done, i - 1)
                        nc.scalar.copy(slotsT[:, i % 2], bank(4 + i % 2)[:, 0:H].rearrange("p (k s) -> p k s", k=KT)
                                       ).then_inc(slotT_ready, 1)
                    if 0 < e <= E:
                        i = l * E + e - 1
                        act.wait_ge(gu_done, i + 1)
                        if i >= 2:
                            act.wait_ge(h_ready, i - 1)
                        nc.scalar.activation(silu_e[:, i % 2, :], bank(i % 2)[:, 0:I], ACT.Silu).then_inc(silu_done, 1)
                    if e >= 3:
                        i = l * E + e - 3
                        act.wait_ge(down_done, i + 1)
                        if i >= 4:
                            act.wait_ge(eo_stored[i % 4], 16 * (i // 4))
                        nc.scalar.copy(eo[(e - 3) % 4], bank(6 + i % 2)[:, 0:H]).then_inc(eo_ready, 1)

        @block.vector
        def _(dve):
            steps = [0]

            def settle(ins):
                steps[0] += 1
                ins.then_inc(dve_step, 1)
                dve.wait_ge(dve_step, steps[0])

            def moments(n, t):
                if n == 0:
                    dve.wait_ge(x_loaded[t], 16)
                settle(nc.vector.bn_stats(stats[:, t, :], x_sb[:, t, :]))
                nc.vector.bn_aggr(meanvar[:, t, :], stats[:, t, :]).then_inc(moments_ready, 1)

            def normalize(n, t):
                dve.wait_ge(rstd_ready, n * NT + t + 1)
                nc.vector.tensor_scalar(xn[:, t, :], x_sb[:, t, :], meanvar[:, t, 0:1], rstd[:, t:t + 1],
                                        ALU.subtract, ALU.mult).then_inc(xn_ready, 1)

            def combine(l, t):
                dve.wait_ge(got[t], 16 * TOPK * (l + 1))
                for k in range(TOPK):
                    last = nc.vector.scalar_tensor_tensor(out=x_sb[:, t, :], in0=gathered[:, k, t, :],
                                                          scalar=topw[:, k, t:t + 1], in1=x_sb[:, t, :],
                                                          op0=ALU.mult, op1=ALU.add)
                    if k == 0:
                        settle(last)
                last.then_inc(layer_done, 1)
                dve.wait_ge(layer_done, l * NT + t + 1)

            def pass1_unit(n, b, unit):
                j, t, _, width, on_diagonal = unit
                dve.wait_ge(s1_done, n + 1)
                if n >= 2:
                    dve.wait_ge(s1_read, n - 1)
                scores = banks[:, b:b + 2, :].rearrange("p b n -> p (b n)")[:, 0:width] if width > HALF else bank(b)[:, 0:width]
                if on_diagonal:
                    nc.vector.tensor_tensor_reduce(
                        out=dump[:, n % 2, 0:width], in0=scores, in1=mask[:, S - width:S], scale=1.0, scalar=NEG,
                        op0=ALU.add, op1=ALU.max, accum_out=rowmax[:, j, t:t + 1]).then_inc(s1_read, 1)
                else:
                    nc.vector.tensor_reduce(out=rowmax_a[:, j, t - NT // 2:t - NT // 2 + 1], in_=scores,
                                            axis=AX.X, op=ALU.max).then_inc(s1_read, 1)

            def routing(l):
                cols = [P, NT, E]

                def wide(a):
                    return a.rearrange("p (t e) -> p t e", e=1).to_broadcast(cols)

                rev = revio[:, :, :].to_broadcast(cols)
                dve.wait_ge(logits_done, (l + 1) * NT)
                settle(nc.vector.tensor_copy(lg[:, :, :], bank(3)[:, 0:NT * E].rearrange("p (t e) -> p t e", t=NT)))
                settle(nc.vector.tensor_reduce(out=s8[:, 0, :], in_=lg[:, :, :], axis=AX.X, op=ALU.max))
                nc.vector.tensor_tensor(tmp[:, :, :], lg[:, :, :], wide(s8[:, 0, :]), ALU.subtract).then_inc(exp_in, 1)
                dve.wait_ge(exp_out, l + 1)
                settle(nc.vector.tensor_reduce(out=s8[:, 0, :], in_=ex[:, :, :], axis=AX.X, op=ALU.add))
                settle(nc.vector.reciprocal(s8[:, 1, :], s8[:, 0, :]))
                settle(nc.vector.tensor_tensor(sc[:, :, :], ex[:, :, :], wide(s8[:, 1, :]), ALU.mult))
                for k in range(TOPK):
                    settle(nc.vector.tensor_reduce(out=topw[:, k, :], in_=sc[:, :, :], axis=AX.X, op=ALU.max))
                    settle(nc.vector.tensor_tensor(tmp[:, :, :], sc[:, :, :], wide(topw[:, k, :]), ALU.is_equal))
                    settle(nc.vector.tensor_tensor(tmp[:, :, :], tmp[:, :, :], rev, ALU.mult))
                    settle(nc.vector.tensor_reduce(out=key[:, k, :], in_=tmp[:, :, :], axis=AX.X, op=ALU.max))
                    settle(nc.vector.tensor_tensor(hot[:, k], rev, wide(key[:, k, :]), ALU.is_equal))
                    if k == 0:
                        settle(nc.vector.scalar_tensor_tensor(out=sc[:, :, :], in0=hot[:, k], scalar=-4.0,
                                                              in1=sc[:, :, :], op0=ALU.mult, op1=ALU.add))
                nc.vector.tensor_tensor(hot_b[:, :, :], hot[:, 0], hot[:, 1], ALU.add).then_inc(hot_ready, 1)
                dve.wait_ge(rank_done, l + 1)
                ranks = bank(2)[:, 0:NT * E].rearrange("p (t e) -> p t e", t=NT)
                for k in range(TOPK):
                    settle(nc.vector.tensor_tensor(tmp[:, :, :], ranks, hot[:, k], ALU.mult))
                    settle(nc.vector.tensor_reduce(out=rank[:, k, :], in_=tmp[:, :, :], axis=AX.X, op=ALU.add))
                nc.vector.tensor_scalar(slot0[:, :, :], key[:, :, :], -float(CAP), float(E * CAP), ALU.mult, ALU.add)
                nc.vector.tensor_scalar(slot1[:, :, :], rank[:, :, :], float(CAP), float(4 * E * CAP), ALU.is_ge, ALU.mult)
                settle(nc.vector.tensor_scalar(slot2[:, :, :], rank[:, :, :], float(CAP - 1), None, ALU.min))
                nc.vector.tensor_tensor(get_at[:, :, :], slot0[:, :, :], slot2[:, :, :], ALU.add)
                settle(nc.vector.tensor_tensor(slot1[:, :, :], slot1[:, :, :], rank[:, :, :], ALU.add))
                nc.vector.tensor_tensor(put_at[:, :, :], slot0[:, :, :], slot1[:, :, :], ALU.add).then_inc(slots_known, 1)

            for l in range(LAYERS):
                for t in range(2):
                    if l > 0:
                        combine(l - 1, t)
                    moments(2 * l, t)
                for t in range(2):
                    normalize(2 * l, t)
                if l == 0:
                    dve.wait_ge(rope_loaded, 16)
                    dve.wait_ge(mask_ready, 1)
                else:
                    dve.wait_ge(maxT_done, l * NG)
                for t in range(NT + 3):
                    if t + 2 < NT:
                        if l > 0:
                            combine(l - 1, t + 2)
                        moments(2 * l, t + 2)
                    if t < NT:
                        i = l * NT + t
                        dve.wait_ge(proj_done, i + 1)
                        if i >= 2:
                            dve.wait_ge(rope_sum, i - 1)
                        qk = bank(2 + i % 2).rearrange("p (h b d) -> p h b d", h=2 * NH, b=2)
                        shape = [P, 2 * NH, 2, HH]

                        def table(m):
                            return rope_sb[:, l, t, m:m + 1, :].rearrange("p o (b d) -> p o b d", b=2).to_broadcast(shape)

                        nc.vector.tensor_tensor(rope_a[i % 2].rearrange("p (h b d) -> p h b d", h=2 * NH, b=2),
                                                qk, table(0), ALU.mult)
                        nc.vector.tensor_tensor(rope_b[i % 2].rearrange("p (h b d) -> p h b d", h=2 * NH, b=2),
                                                qk[:, :, ::-1, :], table(1), ALU.mult).then_inc(rope_mul, 1)
                    if 0 < t <= NT:
                        i = l * NT + t - 1
                        dve.wait_ge(part1_ready, i + 1)
                        r = roped[i % 3].rearrange("p (h d) -> p h d", d=HD)
                        nc.vector.tensor_tensor(r, r, parts[:, i % 3, :, 4, :], ALU.subtract).then_inc(rest_ready, 1)
                    if t + 2 < NT:
                        normalize(2 * l, t + 2)
                    if 1 < t <= NT + 1:
                        i = l * NT + t - 2
                        for c in (0, 2):
                            dve.wait_ge(stackT_done, 4 * i + c + 1)
                            nc.vector.tensor_copy(chunk(c, t - 2), chunk_bank(c)).then_inc(stackT_read_v, 1)
                    if t >= 3:
                        for u, unit in enumerate(NARROW[t - 3]):
                            n = narrow_index(l, t - 3) + u
                            pass1_unit(n, n % 2, unit)
                dve.wait_ge(s1_read, wide_index(l, 1))
                nc.vector.tensor_tensor(rowmax[:, :, NT // 2:], rowmax[:, :, NT // 2:], rowmax_a[:, :, :],
                                        ALU.max).then_inc(max_ready, 1)
                for g in range(1, NG):
                    dve.wait_ge(maxT_done, l * NG + g)
                    for u, unit in enumerate(WIDE):
                        n = wide_index(l, g) + u
                        pass1_unit(n, 2 * (n % 2), unit)
                for t in range(NT + 4):
                    if t < NT:
                        i = l * NT + t
                        dve.wait_ge(oback_done, i + 1)
                        o4 = bank(i % 2).rearrange("p (h w) -> p h w", h=NH)
                        settle(nc.vector.reciprocal(recip[:, i % 2, :], o4[:, :, HD]))
                        if i >= 2:
                            dve.wait_ge(o2T_done, i - 1)
                        nc.vector.tensor_tensor(o_tok[:, i % 2, :].rearrange("p (h d) -> p h d", h=NH), o4[:, :, 0:HD],
                                                recip[:, i % 2, :].rearrange("p (h d) -> p h d", d=1)
                                                .to_broadcast([P, NH, HD]), ALU.mult).then_inc(o_ready, 1)
                    if 3 <= t < NT + 3:
                        i = l * NT + t - 3
                        dve.wait_ge(wo_done, i + 1)
                        nc.vector.tensor_tensor(x_sb[:, t - 3, :], x_sb[:, t - 3, :], bank(4 + i % 2)[:, 0:H],
                                                ALU.add).then_inc(attn_added, 1)
                        dve.wait_ge(attn_added, i + 1)
                        moments(2 * l + 1, t - 3)
                    if t >= 4:
                        normalize(2 * l + 1, t - 4)
                routing(l)
                for m in range(6):
                    i, (m0, mw) = 6 * l + m, IS_TILES[m % 3]
                    dve.wait_ge(shared_silu, i + 1)
                    nc.vector.tensor_tensor(hsT[0:mw, m % 3, (m // 3) * HALF:(m // 3 + 1) * HALF],
                                            silu_s[i % 2][0:mw, :], bank(4 + i % 2)[0:mw, :], ALU.mult).then_inc(shared_h, 1)
                for t in range(NT):
                    i = l * NT + t
                    dve.wait_ge(shared_down, i + 1)
                    nc.vector.tensor_tensor(x_sb[:, t, :], x_sb[:, t, :], bank(6 + i % 2)[:, 0:H],
                                            ALU.add).then_inc(shared_added, 1)
                for e in range(1, E + 2):
                    if e <= E:
                        i = l * E + e - 1
                        dve.wait_ge(silu_done, i + 1)
                        if i >= 2:
                            dve.wait_ge(hT_done, i - 1)
                        nc.vector.tensor_tensor(h_e[:, i % 2, :], silu_e[:, i % 2, :], bank(i % 2)[:, I:2 * I],
                                                ALU.mult).then_inc(h_ready, 1)
                    if e >= 2:
                        i = l * E + e - 2
                        dve.wait_ge(hT_done, i + 1)
                        if i >= 2:
                            dve.wait_ge(down_done, i - 1)
                        nc.vector.tensor_copy(hT_e[:, i % 2], bank(2 + i % 2)[0:IH, 0:2 * P]
                                              .rearrange("p (k s) -> p k s", k=2)).then_inc(hT_ready, 1)
                dve.wait_ge(shared_added, (l + 1) * NT)
            for t in range(NT):
                combine(LAYERS - 1, t)

        @block.tensor
        def _(pe):
            def transposes_xn(n, t, b, copied):
                pe.wait_ge(xn_ready, n * NT + t + 1)
                if copied:
                    pe.wait_ge(xnT_ready, copied)
                for k in range(KT):
                    last = nc.tensor.transpose(bank(b)[:, k * P:(k + 1) * P], xn[:, t, k * P:(k + 1) * P], ident[:, :])
                last.then_inc(xT_done, 1)

            def pass1_unit(l, g, n, b, unit):
                j, t, first, width, _ = unit
                if n >= 2:
                    pe.wait_ge(s1_read, n - 1)
                for c in range(0, width, HALF):
                    w = min(HALF, width - c)
                    last = nc.tensor.matmul(bank(b + c // HALF)[:, 0:w], heads(0, g * GH + j)[0:SR, t * P:(t + 1) * P],
                                            heads(1, g * GH + j)[0:SR, first + c:first + c + w], start=True, stop=True)
                last.then_inc(s1_done, 1)

            def transpose_max(l, g):
                if g == 0:
                    pe.wait_ge(max_ready, l + 1)
                else:
                    pe.wait_ge(s1_read, wide_index(l, g + 1))
                nc.tensor.transpose(bank(0)[0:GH * NT, 0:P], rowmax[:, :, :].rearrange("p h t -> p (h t)"),
                                    ident[:, :]).then_inc(maxT_done, 1)

            def pass2(l, g, s, j):
                qc, kt = STEPS[s]
                first, width = columns(STEPS[s])
                u, h, q0 = 4 * ((l * NG + g) * NS + s) + j, g * GH + j, qc * HALF + first
                if u >= 3:
                    pe.wait_ge(exp_done, u - 2)
                nc.tensor.matmul(bank(4 + u % 3)[:, 0:width], heads(1, h)[0:SA, kt * P:(kt + 1) * P],
                                 heads(0, h)[0:SA, q0:q0 + width], start=True, stop=True).then_inc(s2_done, 1)

            def products_v(l, g, s):
                qc, kt = STEPS[s]
                first, width = columns(STEPS[s])
                n = (l * NG + g) * NS + s
                starts, ends = kt == 0, s in STEP_ENDS
                if starts and n > 0:
                    pe.wait_ge(oT_ready, (l * NG + g) * NQ + qc)
                pe.wait_ge(exp_done, 4 * n + 4)
                if diagonal(STEPS[s]):
                    pe.wait_ge(masked, 2 * ((l * NG + g) * DIAGONALS + sum(diagonal(x) for x in STEPS[:s + 1])))
                for j in range(GH):
                    last = nc.tensor.matmul(bank(7)[VW * j:VW * (j + 1), first:first + width],
                                            v_x[:, kt, g * GH + j, :], probs_all[:, (4 * n + j) % 8, 0:width],
                                            start=starts, stop=ends)
                last.then_inc(pv_done, 1)

            def back(l, t):
                i = l * NT + t
                if i >= 2:
                    pe.wait_ge(o_ready, i - 1)
                for g in range(NG):
                    last = nc.tensor.transpose(bank(i % 2)[:, g * P:(g + 1) * P], oT[:, g, t * P:(t + 1) * P], ident[:, :])
                last.then_inc(oback_done, 1)

            def o_transposes(l, t):
                i = l * NT + t
                pe.wait_ge(o_ready, i + 1)
                if i >= 1:
                    pe.wait_ge(o_T_ready, i)
                for k in range(KT):
                    last = nc.tensor.transpose(bank(2)[:, k * P:(k + 1) * P], o_tok[:, i % 2, k * P:(k + 1) * P],
                                               ident[:, :])
                last.then_inc(o2T_done, 1)

            def o_product(l, t):
                i = l * NT + t
                pe.wait_ge(o_T_ready, i + 1)
                if i >= 2:
                    pe.wait_ge(attn_added, i - 1)
                for k in range(KT):
                    last = nc.tensor.matmul(bank(4 + i % 2)[:, 0:H], o_T[:, i % 2, k, :], wo_sb[:, l, k, :],
                                            start=(k == 0), stop=(k == KT - 1))
                last.then_inc(wo_done, 1)

            pe.wait_ge(consts_ready, 1)
            for l in range(LAYERS):
                if l > 0:
                    pe.wait_ge(eo_ready, l * E)
                transposes_xn(2 * l, 0, 5, 0)
                pe.wait_ge(wqkv_loaded, 16 * (l + 1))
                for t in range(NT + 3):
                    if t + 1 < NT:
                        transposes_xn(2 * l, t + 1, 5, 2 * l * NT + t + 1)
                    if t < NT:
                        i = l * NT + t
                        if t + 1 == NT:
                            pe.wait_ge(xnT_ready, (2 * l + 1) * NT)
                        if i >= 2:
                            pe.wait_ge(rope_mul, i - 1)
                        for k in range(KT):
                            nc.tensor.matmul(bank(2 + i % 2), xnT[:, k, t * P:(t + 1) * P], wqkv_sb[:, k, 0:2 * H],
                                             start=(k == 0), stop=(k == KT - 1))
                        if i >= 1:
                            pe.wait_ge(v_copied, i)
                        for k in range(KT):
                            last = nc.tensor.matmul(bank(4)[:, 0:H], xnT[:, k, t * P:(t + 1) * P],
                                                    wqkv_sb[:, k, 2 * H:3 * H], start=(k == 0), stop=(k == KT - 1))
                        last.then_inc(proj_done, 1)
                    if 1 < t <= NT + 1:
                        i = l * NT + t - 2
                        pe.wait_ge(parts_ready, i + 1)
                        for c in range(4):
                            before_it = 2 * i + c // 2
                            if before_it:
                                pe.wait_ge(stackT_read_a if c % 2 else stackT_read_v, before_it)
                            for h in range(8):
                                last = nc.tensor.transpose(bank(6 + c % 2)[0:SR, :].bitcast(BF16)[:, h * P:(h + 1) * P],
                                                           parts[:, i % 3, 8 * c + h].rearrange("p j d -> p (j d)"), ident_b[:, :])
                            last.then_inc(stackT_done, 1)
                    if t >= 3:
                        pe.wait_ge(stackT_read_v, 2 * (l * NT + t - 2))
                        pe.wait_ge(stackT_read_a, 2 * (l * NT + t - 2))
                        for u, unit in enumerate(NARROW[t - 3]):
                            n = narrow_index(l, t - 3) + u
                            pass1_unit(l, 0, n, n % 2, unit)
                transpose_max(l, 0)
                pe.wait_ge(rope_mul, (l + 1) * NT)
                pe.wait_ge(v_copied, (l + 1) * NT)
                pe.wait_ge(v_fixed, l + 1)
                pe.wait_ge(ones_loaded, 16 * PARTS * NG * (l + 1))
                for g in range(NG):
                    pe.wait_ge(negmax_ready, l * NG + g + 1)
                    pe.wait_ge(shift_loaded, 16 * PARTS * (l * NG + g + 1))
                    for s in range(NS):
                        units = list(wide_units(s)) if g + 1 < NG else []
                        if s == MAX_STEP and g + 1 < NG:
                            transpose_max(l, g + 1)
                        for j in range(GH):
                            pass2(l, g, s, j)
                            for u in units[j * len(units) // GH:(j + 1) * len(units) // GH]:
                                n = wide_index(l, g + 1) + u
                                pass1_unit(l, g + 1, n, 2 * (n % 2), WIDE[u])
                        if s > 0:
                            products_v(l, g, s - 1)
                    products_v(l, g, NS - 1)
                if l == 0:
                    pe.wait_ge(wo_loaded, 16)
                    pe.wait_ge(moe_loaded, 64)
                pe.wait_ge(s1_read, (l + 1) * UNITS)
                pe.wait_ge(oT_ready, (l + 1) * NG * NQ)
                for t in range(NT + 6):
                    if t < NT:
                        back(l, t)
                    if 0 < t <= NT:
                        o_transposes(l, t - 1)
                    if 1 < t <= NT + 1:
                        o_product(l, t - 2)
                    if 5 <= t < NT + 5:
                        b = t - 5
                        transposes_xn(2 * l + 1, b, 6 + b % 2, (2 * l + 1) * NT + b - 1)
                    if t >= 6:
                        b = t - 6
                        pe.wait_ge(xnT_ready, (2 * l + 1) * NT + b + 1)
                        for k in range(KT):
                            last = nc.tensor.matmul(bank(3)[:, b * E:(b + 1) * E], xnT[:, k, b * P:(b + 1) * P],
                                                    gate_sb[:, k, :], start=(k == 0), stop=(k == KT - 1))
                        last.then_inc(logits_done, 1)

                def shared_product(m):
                    i, (m0, mw) = 6 * l + m, IS_TILES[m % 3]
                    if i >= 2:
                        pe.wait_ge(shared_h, i - 1)
                    for b, off in ((0, 0), (4, IS)):
                        for k in range(KT):
                            last = nc.tensor.matmul(bank(b + i % 2)[0:mw, :], wsgu_sb[:, k, off + m0:off + m0 + mw],
                                                    xnT[:, k, (m // 3) * HALF:(m // 3 + 1) * HALF],
                                                    start=(k == 0), stop=(k == KT - 1))
                    last.then_inc(shared_up, 1)

                shared_product(0)
                shared_product(1)
                pe.wait_ge(hot_ready, l + 1)
                nc.tensor.matmul(bank(2)[:, 0:NT * E], before[:, :], hot_b[:, :, :].rearrange("p t e -> p (t e)"),
                                 start=True, stop=False)
                for j in range(NT - 1):
                    last = nc.tensor.matmul(bank(2)[:, (j + 1) * E:NT * E].rearrange("p (t e) -> p t e", e=E),
                                            ones_b[:, :], hot_b[:, j:j + 1, :].to_broadcast([P, NT - 1 - j, E]),
                                            start=False, stop=(j == NT - 2))
                last.then_inc(rank_done, 1)
                for m in range(2, 6):
                    shared_product(m)
                for t in range(NT):
                    i = l * NT + t
                    if t == 0:
                        pe.wait_ge(shared_h, 6 * (l + 1))
                        pe.wait_ge(xnT_ready, (2 * l + 2) * NT)
                    if i >= 2:
                        pe.wait_ge(shared_added, i - 1)
                    for m, (m0, mw) in enumerate(IS_TILES):
                        last = nc.tensor.matmul(bank(6 + i % 2)[:, 0:H], hsT[0:mw, m, t * P:(t + 1) * P], wsd_sb[0:mw, m, :],
                                                start=(m == 0), stop=(m == 2))
                    last.then_inc(shared_down, 1)
                pe.wait_ge(shared_added, (l + 1) * NT)
                pe.wait_ge(slots_known, l + 1)
                for e in range(E + 3):
                    if e < E:
                        i = l * E + e
                        if e % 4 == 0:
                            pe.wait_ge(slots_loaded[e // 4], 16 * (l + 1))
                        if i >= 2:
                            pe.wait_ge(slotT_ready, i - 1)
                        for k in range(KT):
                            last = nc.tensor.transpose(bank(4 + i % 2)[:, k * P:(k + 1) * P], slots[:, e, k * P:(k + 1) * P],
                                                       ident[:, :])
                        last.then_inc(slotT_done, 1)
                    if 0 < e <= E:
                        i = l * E + e - 1
                        pe.wait_ge(slotT_ready, i + 1)
                        pe.wait_ge(expert_loaded[e - 1], 32 * (l + 1))
                        if i >= 2:
                            pe.wait_ge(h_ready, i - 1)
                        for k in range(KT):
                            last = nc.tensor.matmul(bank(i % 2)[:, 0:2 * I], slotsT[:, i % 2, k, :], wgu_sb[:, e - 1, k, :],
                                                    start=(k == 0), stop=(k == KT - 1))
                        last.then_inc(gu_done, 1)
                    if 1 < e <= E + 1:
                        i = l * E + e - 2
                        pe.wait_ge(h_ready, i + 1)
                        if i >= 2:
                            pe.wait_ge(hT_ready, i - 1)
                        for k in range(2):
                            last = nc.tensor.transpose(bank(2 + i % 2)[0:IH, k * P:(k + 1) * P],
                                                       h_e[:, i % 2, k * IH:(k + 1) * IH], ident[:, :])
                        last.then_inc(hT_done, 1)
                    if e > 2:
                        i = l * E + e - 3
                        pe.wait_ge(hT_ready, i + 1)
                        if i >= 2:
                            pe.wait_ge(eo_ready, i - 1)
                        for k in range(2):
                            last = nc.tensor.matmul(bank(6 + i % 2)[:, 0:H], hT_e[:, i % 2, k, :], wd_sb[:, e - 3, k, :],
                                                    start=(k == 0), stop=(k == 1))
                        last.then_inc(down_done, 1)


def rope_tables():
    inv_freq = (1.0 / 10000.0 ** (np.arange(0, HD, 2, dtype=np.float32) / HD)).astype(np.float32)
    freqs = np.einsum("i,j->ij", np.arange(S, dtype=np.float32), inv_freq)
    cos, sin = np.cos(freqs).astype(np.float32), np.sin(freqs).astype(np.float32)
    rows = []
    for a, b in ((cos, sin), (sin, cos)):
        rows.append(np.stack([np.concatenate([a, a], 1), np.concatenate([-b, b], 1)], 1))
    table = np.stack(rows)
    return np.ascontiguousarray(table.reshape(LAYERS, NT, P, 2, HD).transpose(2, 0, 1, 3, 4))


def kernel(**inputs):
    import numpy as _np
    import concourse.bacc as _bacc
    from concourse import mybir as _mybir
    from concourse.bass_utils import run_bass_kernel_spmd as _run

    a = {k: _np.asarray(v) for k, v in inputs.items()}

    def qkv(which):
        return _np.concatenate([a[f"L0_attn_{which}_W{m}"].T for m in "qkv"], axis=1)

    arrays = {
        "x": a["L0_attn_a_hidden_states"].reshape(S, H),
        "wqkv": _np.stack([qkv("a"), qkv("b")]),
        "wo": _np.stack([a["L0_attn_a_Wo"].T, a["L0_attn_b_Wo"].T]),
        "gate": a["L0_ffn_gate_w"].T,
        "wgu": _np.concatenate([a["L0_ffn_w_gate"], a["L0_ffn_w_up"]], axis=2),
        "wdown": a["L0_ffn_w_down"],
        "wsgu": _np.concatenate([a["L0_ffn_ws_gate"], a["L0_ffn_ws_up"]], axis=1),
        "wsdown": a["L0_ffn_ws_down"],
        "rope": rope_tables(),
    }
    nc = _bacc.Bacc("TRN2", target_bir_lowering=False, num_devices=1)
    feeds, args = {}, []
    for name, value in arrays.items():
        feeds[f"{name}_dram"] = _np.ascontiguousarray(value)
        args.append(nc.dram_tensor(f"{name}_dram", value.shape, _mybir.dt.from_np(value.dtype), kind="ExternalInput").ap())
    args.append(nc.dram_tensor("out_dram", (S, H), _mybir.dt.float32, kind="ExternalOutput").ap())
    build(nc, *args)
    r = _run(nc, [feeds], core_ids=[0])
    return r.results[0]["out_dram"].reshape(1, S, H)
```

```python
import numpy as np
from contextlib import ExitStack

import concourse.bass as bass
from concourse import mybir

F32 = mybir.dt.float32
BF16 = mybir.dt.bfloat16
U32 = mybir.dt.uint32
ALU = mybir.AluOpType
ACT = mybir.ActivationFunctionType
AX = mybir.AxisListType

P = 128
S = 1024
NT = S // P
H = 256
KT = H // P
NH = 16
HD = H // NH
HH = HD // 2
LAYERS = 2
GH = 4
NG = NH // GH
PARTS = 3
NB = 6
SR = NB * HD
SA = SR + PARTS
VW = 32
HALF = 512
NQ = S // HALF
E = 16
CAP = 128
TOPK = 2
I = 176
IH = I // 2
IS = 352
IS_TILES = [(0, 128), (128, 128), (256, 96)]
EPS = 1e-5
NEG = -3.0e38
EXPERT_WORDS = KT * 2 * I + 2 * H
GROUP_WORDS = GH * S
FREED = [min(E, (g + 1) * GROUP_WORDS // EXPERT_WORDS) for g in range(NG - 1)] + [E]

STEPS = [(0, 0), (0, 1), (0, 2), (0, 3), (1, 0), (1, 4), (1, 5), (1, 6), (1, 7), (1, 1), (1, 2), (1, 3)]
NS = len(STEPS)
STEP_ENDS = {3: 0, 11: 1}

TILE_UNITS = [[] for _ in range(NT)]
for t in range(NT):
    keys = (t + 1) * P
    for j in range(GH):
        if keys > HALF:
            TILE_UNITS[t].append((j, t, 0, HALF, False))
            TILE_UNITS[t].append((j, t, HALF, keys - HALF, True))
        else:
            TILE_UNITS[t].append((j, t, 0, keys, True))
ALL_UNITS = sum(TILE_UNITS, [])
GU = len(ALL_UNITS)
UNITS = NG * GU
LAST_TILES = 6
TWO_BANKS = sum(map(len, TILE_UNITS[:LAST_TILES]))

DVE_CHUNKS = 5
GATHERED = 5
PV_LAG = 2
CLOCK_START = 45
CLOCK_TAIL = 6
MAX_STEP = 9


def diagonal(step):
    qc, kt = step
    return kt * P >= qc * HALF


DIAGONALS = sum(diagonal(s) for s in STEPS)


def columns(step):
    qc, kt = step
    first = max(kt * P - qc * HALF, 0)
    return first, HALF - first


STEP_FIXED = 128
UNIT_FIXED = 128
WORK = np.cumsum([0] + [columns(x)[1] + STEP_FIXED for x in STEPS])
KEYS = np.cumsum([0] + [u[3] + UNIT_FIXED for u in ALL_UNITS] * (NG - 1))
EARLY = 18
EARLIEST = 2


def later_until(g, s):
    knots = [(0, EARLY)] + [(i * WORK[-1] + WORK[MAX_STEP], (i + 1) * GU) for i in range(NG - 1)]
    keys = np.interp(g * WORK[-1] + WORK[s], [k[0] for k in knots], [KEYS[k[1]] for k in knots])
    return int(np.searchsorted(KEYS, keys - 0.5))


def later_units(g, s):
    return range(later_until(g, s), later_until(g, s + 1))


def quarter(units, n):
    return units[n * len(units) // 4:(n + 1) * len(units) // 4]


def max_turns(g, s):
    return 1 + min(g + (s >= MAX_STEP), NG - 1)


ROT = NG + NG * NS * 2


def build(nc, x, wqkv, wo, gate, wgu, wdown, wsgu, wsdown, rope, out):
    ctx = ExitStack()
    with ctx:
        def sb(name, shape, dt=F32):
            return ctx.enter_context(nc.sbuf_tensor(name, shape, dt))

        def sem(name):
            return ctx.enter_context(nc.semaphore(name))

        x_sb = sb("x_sb", [P, NT, H])
        norms = sb("norms", [P, 2 * NT * H])
        xn = norms[:, 0:NT * H].rearrange("p (t d) -> p t d", t=NT)
        xnT = norms[:, NT * H:2 * NT * H].rearrange("p (k s) -> p k s", k=KT)
        oT = norms[:, :].rearrange("p (g s) -> p g s", g=NG)
        QKW, VWORDS = NG * GROUP_WORDS, NT * NH * VW
        arena = sb("arena", [P, QKW + VWORDS])
        qk_st = arena[:, 0:QKW].bitcast(BF16).rearrange("p (g b h s) -> p g b h s", g=NG, b=2, h=GH)
        v_x = arena[:, QKW:].rearrange("p (t h w) -> p t h w", t=NT, h=NH)
        GUW = KT * 2 * I
        experts = arena[:, 0:E * EXPERT_WORDS].rearrange("p (e w) -> p e w", e=E)
        wgu_sb = experts[:, :, 0:GUW].rearrange("p e (k n) -> p e k n", k=KT)
        wd_sb = experts[0:IH, :, GUW:EXPERT_WORDS].rearrange("p e (k n) -> p e k n", k=2)
        stage = sb("stage", [P, 7 * 2 * H])
        rope_a = [stage[:, 1024 * b:1024 * b + 512] for b in range(2)]
        rope_b = [stage[:, 1024 * b + 512:1024 * b + 1024] for b in range(2)]
        roped = [stage[:, 2048 + 512 * b:2560 + 512 * b] for b in range(3)]
        silu_s = [stage[:, 512 * b:512 * b + 512] for b in range(2)]
        eo = [stage[:, 1024 + 256 * b:1280 + 256 * b] for b in range(4)]
        parts_all = sb("parts_all", [P, 3 * NH * NB * HD])
        parts = parts_all[:, :].bitcast(BF16).rearrange("p (b h j d) -> p b h j d", b=3, h=2 * NH, j=NB)
        hsT = parts_all[:, 0:3 * S].rearrange("p (m s) -> p m s", m=3)
        probs_all = sb("probs", [P, 8, HALF])
        probs_more = stage[:, 0:4 * HALF].rearrange("p (b n) -> p b n", b=4)
        slots = probs_all[:, :, :].rearrange("p a (b d) -> p (a b) d", d=H)
        gathered = slots.rearrange("p (k t) d -> p k t d", k=TOPK)
        wqkv_sb = sb("wqkv_sb", [P, KT, 3 * H])
        wo_sb = sb("wo_sb", [P, LAYERS, KT, H])
        gate_sb = sb("gate_sb", [P, KT, E])
        wsgu_sb = sb("wsgu_sb", [P, KT, 2 * IS])
        wsd_sb = sb("wsd_sb", [P, 3, H])
        rope_sb = sb("rope_sb", [P, LAYERS, NT, 2, HD])
        ident = sb("ident", [P, P])
        ident_b = sb("ident_b", [P, P], BF16)
        before = sb("before", [P, P], BF16)
        ones_b = sb("ones_b", [P, P], BF16)
        mask = sb("mask", [P, HALF], BF16)
        revio = sb("revio", [P, 1, E])
        revio_i = sb("revio_i", [P, E], mybir.dt.int32)
        neghalf = sb("neghalf", [P, NT])
        stats = sb("stats", [P, NT, 6])
        meanvar = sb("meanvar", [P, NT, 2])
        vareps = sb("vareps", [P, NT])
        rstd = sb("rstd", [P, NT])
        dump = sb("dump", [P, 2, HALF], BF16)
        rowmax = sb("rowmax", [P, 2, GH, NT])
        rowmax_a = sb("rowmax_a", [P, 2, GH, NT // 2])
        negmax = sb("negmax", [GH * NT, P])
        negrest = sb("negrest", [GH * NT, P])
        shift = sb("shift", [GH * NT, PARTS, P], BF16)
        recip = sb("recip", [P, 2, NH])
        o_tok = sb("o_tok", [P, 2, H])
        o_T = sb("o_T", [P, 2, KT, P])
        slotsT = sb("slotsT", [P, 2, KT, P])
        silu_e = sb("silu_e", [P, 2, I])
        h_e = sb("h_e", [P, 2, I])
        hT_e = sb("hT_e", [IH, 2, 2, P])
        lg = sb("lg", [P, NT, E])
        ex = sb("ex", [P, NT, E])
        sc = sb("sc", [P, NT, E])
        tmp = sb("tmp", [P, NT, E])
        hot = sb("hot", [P, TOPK, NT, E])
        hot_b = sb("hot_b", [P, NT, E], BF16)
        s8 = sb("s8", [P, 2, NT])
        topw = sb("topw", [P, TOPK, NT])
        key = sb("key", [P, TOPK, NT])
        rank = sb("rank", [P, TOPK, NT])
        slot0 = sb("slot0", [P, TOPK, NT])
        slot1 = sb("slot1", [P, TOPK, NT])
        slot2 = sb("slot2", [P, TOPK, NT])
        put_at = sb("put_at", [P, TOPK, NT], U32)
        get_at = sb("get_at", [P, TOPK, NT], U32)
        zeros = o_tok[:, :, :]

        slots_dram = nc.dram_tensor("slots_dram", (E * CAP, H), F32, kind="Internal").ap()
        eo_dram = nc.dram_tensor("eo_dram", (E * CAP, H), F32, kind="Internal").ap()

        banks = ctx.enter_context(nc.psum_tensor("banks", [P, 8, HALF], F32))

        def bank(n):
            return banks[:, n, :]

        def probs(n, pair):
            place = 2 * (n % 3) + pair
            return probs_all[:, 2 * place:2 * place + 2, :] if place < 4 else probs_more[:, 2 * place - 8:2 * place - 6, :]

        def pass1_bank(n):
            u = n % UNITS
            return (u % 2, 2) if u < TWO_BANKS else ((u - TWO_BANKS) % 3, 2 if u < TWO_BANKS + 2 else 3)

        def pass2_bank(use):
            return 3 + 2 * (use % 2)


        def heads(b, h):
            return qk_st[:, h // GH, b, h % GH, :]

        def chunk(c, t):
            return qk_st[0:SR, 2 * (c % 2):2 * (c % 2) + 2, c // 2, :, t * P:(t + 1) * P]

        def chunk_bank(c):
            return bank(6 + c % 2)[0:SR, :].bitcast(BF16).rearrange("p (g h s) -> p g h s", g=2, h=GH)

        def first_units(l, t):
            return list(enumerate(TILE_UNITS[t], l * UNITS + sum(len(x) for x in TILE_UNITS[:t])))

        def later_index(l, w):
            return l * UNITS + GU + w

        def use_of(l, g, s, pair):
            return l * ROT + max_turns(g, s) + (g * NS + s) * 2 + pair

        def turn_of(l, g):
            return l * ROT if g == 0 else use_of(l, g - 1, MAX_STEP, 0) - 1

        x_loaded = [sem(f"x_loaded{t}") for t in range(NT)]
        wqk_loaded = sem("wqk_loaded")
        wv_loaded = sem("wv_loaded")
        wo_loaded = sem("wo_loaded")
        rope_loaded = sem("rope_loaded")
        moe_loaded = sem("moe_loaded")
        ones_ready = sem("ones_ready")
        consts_ready = sem("consts_ready")
        mask_ready = sem("mask_ready")
        zeros_ready = sem("zeros_ready")
        slots_zeroed = sem("slots_zeroed")
        moments_ready = sem("moments_ready")
        ones_loaded = sem("ones_loaded")
        rstd_ready = sem("rstd_ready")
        xn_ready = sem("xn_ready")
        xT_done = sem("xT_done")
        xnT_ready = sem("xnT_ready")
        proj_done = sem("proj_done")
        qk_done = sem("qk_done")
        rope_mul = sem("rope_mul")
        rope_sum = sem("rope_sum")
        part1_ready = sem("part1_ready")
        rest_ready = sem("rest_ready")
        part2_ready = sem("part2_ready")
        parts_ready = sem("parts_ready")
        stackT_done = sem("stackT_done")
        stackT_read = [sem("stackT_read_even"), sem("stackT_read_odd")]
        v_copied = sem("v_copied")
        v_fixed = sem("v_fixed")
        s1_done = sem("s1_done")
        s1_read = sem("s1_read")
        max_ready = sem("max_ready")
        shift_ready = sem("shift_ready")
        shift_loaded = sem("shift_loaded")
        s2_done = sem("s2_done")
        s2_read = sem("s2_read")
        masked = sem("masked")
        pv_done = sem("pv_done")
        oT_ready = sem("oT_ready")
        oback_done = sem("oback_done")
        o_ready = sem("o_ready")
        o2T_done = sem("o2T_done")
        o_T_ready = sem("o_T_ready")
        wo_done = sem("wo_done")
        attn_added = sem("attn_added")
        logits_done = sem("logits_done")
        logits_read = sem("logits_read")
        exp_in = sem("exp_in")
        exp_out = sem("exp_out")
        hot_ready = sem("hot_ready")
        rank_done = sem("rank_done")
        rank_read = sem("rank_read")
        slots_known = sem("slots_known")
        scattered = sem("scattered")
        slots_loaded = [sem(f"slots_loaded{n}") for n in range(4)]
        shared_up = sem("shared_up")
        shared_silu = sem("shared_silu")
        shared_h = sem("shared_h")
        shared_down = sem("shared_down")
        shared_added = sem("shared_added")
        expert_loaded = [sem(f"expert_loaded{e}") for e in range(E)]
        slotT_done = sem("slotT_done")
        slotT_ready = sem("slotT_ready")
        gu_done = sem("gu_done")
        silu_done = sem("silu_done")
        h_ready = sem("h_ready")
        hT_done = sem("hT_done")
        hT_ready = sem("hT_ready")
        down_done = sem("down_done")
        eo_ready = sem("eo_ready")
        eo_stored = [sem(f"eo_stored{n}") for n in range(4)]
        got = [sem(f"got{t}") for t in range(NT)]
        layer_done = sem("layer_done")
        out_stored = sem("out_stored")
        dve_step = sem("dve_step")
        pool_step = sem("pool_step")

        block = ctx.enter_context(nc.Block())

        @block.sync
        def _(sp):
            def load_x(t):
                sp.dma_start(x_sb[:, t, :], x[t * P:(t + 1) * P, :]).then_inc(x_loaded[t], 16)

            load_x(0)
            load_x(1)
            sp.dma_start(wqkv_sb[:, :, 2 * H:], wqkv[0][:, 2 * H:].rearrange("(k p) n -> p k n", p=P)).then_inc(wv_loaded, 16)
            sp.dma_start(rope_sb[:, :, :, :, :], rope).then_inc(rope_loaded, 16)
            for t in range(2, NT):
                load_x(t)
            sp.dma_start(wo_sb[:, :, :, :], wo.rearrange("l (k p) n -> p l k n", p=P)).then_inc(wo_loaded, 16)
            sp.dma_start(gate_sb[:, :, :], gate.rearrange("(k p) e -> p k e", p=P)).then_inc(moe_loaded, 16)
            sp.dma_start(wsgu_sb[:, :, :], wsgu.rearrange("(k p) n -> p k n", p=P)).then_inc(moe_loaded, 16)
            sp.dma_start(wsd_sb[:, 0:2, :], wsdown[0:2 * P, :].rearrange("(k p) n -> p k n", p=P)).then_inc(moe_loaded, 16)
            sp.dma_start(wsd_sb[0:IS - 2 * P, 2, :], wsdown[2 * P:IS, :]).then_inc(moe_loaded, 16)
            sp.wait_ge(zeros_ready, 1)
            for n in range(8):
                sp.dma_start(slots_dram[n * 2 * P:(n + 1) * 2 * P, :].rearrange("(k p) d -> p k d", p=P),
                             zeros).then_inc(slots_zeroed, 16)

            def load_experts(l, g):
                sp.wait_ge(pv_done, (l * NG + g + 1) * NS)
                for e in range(FREED[g - 1] if g else 0, FREED[g]):
                    sp.dma_start(wgu_sb[:, e, :, :], wgu[e].rearrange("(k p) n -> p k n", p=P)).then_inc(expert_loaded[e], 16)
                    sp.dma_start(wd_sb[:, e, :, :], wdown[e].rearrange("(k p) n -> p k n", p=IH)).then_inc(expert_loaded[e], 16)

            for l in range(LAYERS):
                if l == 0:
                    sp.wait_ge(consts_ready, 1)
                else:
                    sp.wait_ge(down_done, l * E)
                for g in range(NG):
                    for part in range(PARTS):
                        sp.dma_start(qk_st[SR + part:SR + part + 1, g, 1], ones_b[0:GH * NT, :]).then_inc(ones_loaded, 16)
                for g in range(NG):
                    sp.wait_ge(shift_ready, l * NG + g + 1)
                    for part in range(PARTS):
                        sp.dma_start(qk_st[SR + part:SR + part + 1, g, 0], shift[:, part, :]).then_inc(shift_loaded, 16)
                    if g > 0:
                        load_experts(l, g - 1)
                load_experts(l, NG - 1)
                if l + 1 < LAYERS:
                    sp.wait_ge(proj_done, NT * (l + 1))
                    sp.dma_start(wqkv_sb[:, :, 0:2 * H], wqkv[l + 1][:, 0:2 * H].rearrange("(k p) n -> p k n", p=P)).then_inc(wqk_loaded, 16)
                    sp.dma_start(wqkv_sb[:, :, 2 * H:], wqkv[l + 1][:, 2 * H:].rearrange("(k p) n -> p k n", p=P)).then_inc(wv_loaded, 16)
                sp.wait_ge(scattered, (l + 1) * TOPK * NT * 16)
                for n in range(4):
                    sp.dma_start(slots[:, 4 * n:4 * n + 4, :],
                                 slots_dram[n * 4 * P:(n + 1) * 4 * P, :].rearrange("(e p) d -> p e d", p=P)
                                 ).then_inc(slots_loaded[n], 16)
                for e in range(E):
                    sp.wait_ge(eo_ready, l * E + e + 1)
                    sp.dma_start(eo_dram[e * CAP:(e + 1) * CAP, :], eo[e % 4]).then_inc(eo_stored[e % 4], 16)
            for t in range(NT):
                sp.wait_ge(layer_done, (LAYERS - 1) * NT + t + 1)
                sp.dma_start(out[t * P:(t + 1) * P, :], x_sb[:, t, :]).then_inc(out_stored, 16)
            sp.wait_ge(out_stored, 16 * NT)

        @block.gpsimd
        def _(pool):
            steps = [0]

            def settle(ins):
                steps[0] += 1
                ins.then_inc(pool_step, 1)
                pool.wait_ge(pool_step, steps[0])

            nc.gpsimd.memset(ones_b[:, :], 1.0).then_inc(ones_ready, 1)
            nc.gpsimd.memset(neghalf[:, :], -0.5)
            nc.gpsimd.memset(zeros, 0.0).then_inc(zeros_ready, 1)
            nc.gpsimd.memset(ident[:, :], 0.0)
            nc.gpsimd.memset(before[:, :], 1.0)
            nc.gpsimd.iota(revio_i[:, :], pattern=[[-1, E]], base=E, channel_multiplier=0)
            settle(nc.gpsimd.memset(mask[:, :], 0.0))
            nc.gpsimd.tensor_copy(revio[:, 0, :], revio_i[:, :])
            settle(nc.gpsimd.affine_select(out=ident[:, :], in_=ident[:, :], compare_op=ALU.not_equal, fill=1.0,
                                           base=0, pattern=[[-1, P]], channel_multiplier=1))
            nc.gpsimd.tensor_copy(ident_b[:, :], ident[:, :])
            nc.gpsimd.affine_select(out=before[:, :], in_=before[:, :], compare_op=ALU.is_gt, fill=0.0,
                                    base=0, pattern=[[1, P]], channel_multiplier=-1).then_inc(consts_ready, 1)
            nc.gpsimd.affine_select(out=mask[:, HALF - P:HALF], in_=mask[:, HALF - P:HALF],
                                    compare_op=ALU.is_ge, fill=NEG, base=0, pattern=[[-1, P]],
                                    channel_multiplier=1).then_inc(mask_ready, 1)

            def deviation(n, t):
                i = n * NT + t
                pool.wait_ge(moments_ready, i + 1)
                settle(nc.gpsimd.tensor_scalar(vareps[:, t:t + 1], meanvar[:, t, 1:2], EPS, None, ALU.add))
                nc.gpsimd.tensor_tensor(rstd[:, t:t + 1], vareps[:, t:t + 1], neghalf[:, 0:1], ALU.pow).then_inc(rstd_ready, 1)

            def causal(l, g, s):
                n = (l * NG + g) * NS + s
                if diagonal(STEPS[s]):
                    for pair in range(2):
                        pool.wait_ge(s2_read, use_of(l, g, s, pair) + 1)
                        blocks = probs(n, pair)[:, :, 0:P]
                        nc.gpsimd.affine_select(out=blocks, in_=blocks, compare_op=ALU.is_ge, fill=0.0, base=0,
                                                pattern=[[0, 2], [1, P]], channel_multiplier=-1).then_inc(masked, 1)

            def split_max(l, g):
                pool.wait_ge(s2_read, turn_of(l, g) + 1)
                settle(nc.gpsimd.tensor_tensor(negrest[:, :], negmax[:, :], shift[:, 0, :], ALU.subtract))
                settle(nc.gpsimd.tensor_copy(shift[:, 1, :], negrest[:, :]))
                nc.gpsimd.tensor_tensor(shift[:, 2, :], negrest[:, :], shift[:, 1, :], ALU.subtract).then_inc(shift_ready, 1)

            def gather(l, t):
                for k in range(TOPK):
                    nc.gpsimd.indirect_dma_start(
                        out=gathered[:, k, t, :], out_offset=None, in_=eo_dram,
                        in_offset=bass.IndirectOffsetOnAxis(ap=get_at[:, k, t:t + 1], axis=0)
                    ).then_inc(got[t], 16)

            for l in range(LAYERS):
                if l > 0:
                    for t in range(2):
                        gather(l - 1, t)
                for t in range(3):
                    if l > 0:
                        gather(l - 1, t + 2)
                    deviation(2 * l, t)
                if l > 0:
                    for t in range(5, GATHERED):
                        gather(l - 1, t)
                for t in range(NT + 1):
                    if t < NT:
                        i = l * NT + t
                        pool.wait_ge(rope_mul, i + 1)
                        if i >= 3:
                            pool.wait_ge(parts_ready, i - 2)
                        nc.gpsimd.tensor_tensor(roped[i % 3], rope_a[i % 2], rope_b[i % 2], ALU.add).then_inc(rope_sum, 1)
                    if t > 0:
                        i = l * NT + t - 1
                        pool.wait_ge(part2_ready, i + 1)
                        rest, to = roped[i % 3].rearrange("p (h d) -> p h d", d=HD), parts[:, i % 3]
                        nc.gpsimd.tensor_tensor(to[:, 0:NH, 5, :], rest[:, 0:NH], to[:, 0:NH, 1, :], ALU.subtract)
                        nc.gpsimd.tensor_tensor(to[:, NH:, 2, :], rest[:, NH:], to[:, NH:, 1, :],
                                                ALU.subtract).then_inc(parts_ready, 1)
                    if l > 0 and t + GATHERED < NT:
                        gather(l - 1, t + GATHERED)
                    if t + 3 < NT:
                        deviation(2 * l, t + 3)
                nc.gpsimd.memset(v_x[:, :, :, HD + 1:VW], 0.0)
                nc.gpsimd.memset(v_x[:, :, :, HD:HD + 1], 1.0).then_inc(v_fixed, 1)
                pool.wait_ge(v_fixed, l + 1)
                split_max(l, 0)
                for g in range(NG):
                    for s in range(NS):
                        if s == MAX_STEP and g + 1 < NG:
                            split_max(l, g + 1)
                        causal(l, g, s)
                for t in range(NT):
                    deviation(2 * l + 1, t)
                pool.wait_ge(slots_known, l + 1)
                if l == 0:
                    pool.wait_ge(slots_zeroed, 16 * 8)
                else:
                    for n in range(4):
                        pool.wait_ge(slots_loaded[n], 16 * l)
                for t in range(NT):
                    for k in range(TOPK):
                        nc.gpsimd.indirect_dma_start(
                            out=slots_dram, out_offset=bass.IndirectOffsetOnAxis(ap=put_at[:, k, t:t + 1], axis=0),
                            in_=xn[:, t, :], in_offset=None, bounds_check=E * CAP - 1, oob_is_err=False
                        ).then_inc(scattered, 16)
                for n in range(4):
                    pool.wait_ge(eo_stored[n], 16 * (l + 1) * E // 4)
            for t in range(NT):
                gather(LAYERS - 1, t)

        @block.scalar
        def _(act):
            act.dma_start(wqkv_sb[:, :, 0:2 * H], wqkv[0][:, 0:2 * H].rearrange("(k p) n -> p k n", p=P)).then_inc(wqk_loaded, 16)

            def copy_xT(n, t, b):
                act.wait_ge(xT_done, n * NT + t + 1)
                nc.scalar.copy(xnT[:, :, t * P:(t + 1) * P],
                               bank(b)[:, 0:H].rearrange("p (k s) -> p k s", k=KT)).then_inc(xnT_ready, 1)

            def copy_chunk(i, c, t):
                act.wait_ge(stackT_done, 4 * i + c + 1)
                nc.scalar.copy(chunk(c, t), chunk_bank(c)).then_inc(stackT_read[c % 2], 1)

            def copy_v(l, t):
                act.wait_ge(proj_done, l * NT + t + 1)
                nc.scalar.copy(v_x[:, t, :, 0:HD], bank(4)[:, 0:H].rearrange("p (h d) -> p h d", h=NH)
                               ).then_inc(v_copied, 1)

            def exps(l, g, s):
                n = (l * NG + g) * NS + s
                first, width = columns(STEPS[s])
                if n >= 3:
                    act.wait_ge(pv_done, n - 2)
                for pair in range(2):
                    u = use_of(l, g, s, pair)
                    act.wait_ge(s2_done, u + 1)
                    nc.scalar.activation(probs(n, pair)[:, :, 0:width], banks[:, pass2_bank(u):pass2_bank(u) + 2, 0:width],
                                         ACT.Exp, scale=HD ** -0.5).then_inc(s2_read, 1)

            def copy_oT(l, g, qc):
                end = [s for s in STEP_ENDS if STEP_ENDS[s] == qc][0]
                act.wait_ge(pv_done, (l * NG + g) * NS + end + 1)
                nc.scalar.copy(oT[:, g, qc * HALF:(qc + 1) * HALF], bank(7)).then_inc(oT_ready, 1)

            def negate_max(l, g):
                n, u = l * NG + g, turn_of(l, g)
                act.wait_ge(s2_done, u + 1)
                if n:
                    act.wait_ge(shift_ready, n)
                    act.wait_ge(shift_loaded, 16 * PARTS * n)
                nc.scalar.mul(negmax[:, :], bank(pass2_bank(u))[0:GH * NT, 0:P], -1.0)
                nc.scalar.mul(shift[:, 0, :], bank(pass2_bank(u))[0:GH * NT, 0:P], -1.0).then_inc(s2_read, 1)

            for l in range(LAYERS):
                for t in range(2):
                    copy_xT(2 * l, t, 5)
                for t in range(NT + 2):
                    if 0 < t <= NT:
                        i = l * NT + t - 1
                        act.wait_ge(rest_ready, i + 1)
                        rest, to = roped[i % 3].rearrange("p (h j d) -> p h j d", j=1, d=HD), parts[:, i % 3]
                        nc.scalar.copy(to[:, 0:NH, 1:4:2, :], rest[:, 0:NH].to_broadcast([P, NH, 2, HD]))
                        nc.scalar.copy(to[:, NH:, 0:2, :], rest[:, NH:].to_broadcast([P, NH, 2, HD])).then_inc(part2_ready, 1)
                    if t > 1:
                        if t - 2 >= DVE_CHUNKS:
                            copy_chunk(l * NT + t - 2, 0, t - 2)
                        copy_chunk(l * NT + t - 2, 1, t - 2)
                    if t < 2:
                        copy_v(l, t)
                    if t < NT:
                        i = l * NT + t
                        act.wait_ge(rope_sum, i + 1)
                        if i >= 3:
                            act.wait_ge(stackT_done, 4 * (i - 2))
                        whole, to = roped[i % 3].rearrange("p (h j d) -> p h j d", j=1, d=HD), parts[:, i % 3]
                        nc.scalar.copy(to[:, 0:NH, 0:5:2, :], whole[:, 0:NH].to_broadcast([P, NH, 3, HD]))
                        nc.scalar.copy(to[:, NH:, 3:6, :], whole[:, NH:].to_broadcast([P, NH, 3, HD])).then_inc(part1_ready, 1)
                    if t > 1:
                        if t - 2 >= DVE_CHUNKS:
                            copy_chunk(l * NT + t - 2, 2, t - 2)
                        copy_chunk(l * NT + t - 2, 3, t - 2)
                    if 2 <= t < NT:
                        copy_v(l, t)
                    if t + 2 < NT:
                        copy_xT(2 * l, t + 2, 5)
                negate_max(l, 0)
                for g in range(NG):
                    for s in range(NS):
                        if s == MAX_STEP and g + 1 < NG:
                            negate_max(l, g + 1)
                        exps(l, g, s)
                        if s - PV_LAG in STEP_ENDS:
                            copy_oT(l, g, STEP_ENDS[s - PV_LAG])
                        if s == PV_LAG - 1 and g > 0:
                            copy_oT(l, g - 1, 1)
                copy_oT(l, NG - 1, 1)
                for t in range(NT + 5):
                    if 0 < t <= NT:
                        i = l * NT + t - 1
                        act.wait_ge(o2T_done, i + 1)
                        if i >= 2:
                            act.wait_ge(wo_done, i - 1)
                        nc.scalar.copy(o_T[:, i % 2], bank(2)[:, 0:H].rearrange("p (k s) -> p k s", k=KT)
                                       ).then_inc(o_T_ready, 1)
                    if t >= 5:
                        copy_xT(2 * l + 1, t - 5, 6 + (t - 5) % 2)
                act.wait_ge(exp_in, l + 1)
                nc.scalar.activation(ex[:, :, :], tmp[:, :, :], ACT.Exp).then_inc(exp_out, 1)
                for m in range(6):
                    i, (_, mw) = 6 * l + m, IS_TILES[m % 3]
                    act.wait_ge(shared_up, i + 1)
                    if i >= 2:
                        act.wait_ge(shared_h, i - 1)
                    nc.scalar.activation(silu_s[i % 2][0:mw, :], bank(i % 2)[0:mw, :], ACT.Silu).then_inc(shared_silu, 1)
                for e in range(E + 3):
                    if e < E:
                        i = l * E + e
                        act.wait_ge(slotT_done, i + 1)
                        if i >= 2:
                            act.wait_ge(gu_done, i - 1)
                        nc.scalar.copy(slotsT[:, i % 2], bank(4 + i % 2)[:, 0:H].rearrange("p (k s) -> p k s", k=KT)
                                       ).then_inc(slotT_ready, 1)
                    if 0 < e <= E:
                        i = l * E + e - 1
                        act.wait_ge(gu_done, i + 1)
                        if i >= 2:
                            act.wait_ge(h_ready, i - 1)
                        nc.scalar.activation(silu_e[:, i % 2, :], bank(i % 2)[:, 0:I], ACT.Silu).then_inc(silu_done, 1)
                    if e >= 3:
                        i = l * E + e - 3
                        act.wait_ge(down_done, i + 1)
                        if i >= 4:
                            act.wait_ge(eo_stored[i % 4], 16 * (i // 4))
                        nc.scalar.copy(eo[(e - 3) % 4], bank(6 + i % 2)[:, 0:H]).then_inc(eo_ready, 1)

        @block.vector
        def _(dve):
            steps = [0]

            def settle(ins):
                steps[0] += 1
                ins.then_inc(dve_step, 1)
                dve.wait_ge(dve_step, steps[0])

            def moments(n, t):
                if n == 0:
                    dve.wait_ge(x_loaded[t], 16)
                settle(nc.vector.bn_stats(stats[:, t, :], x_sb[:, t, :]))
                nc.vector.bn_aggr(meanvar[:, t, :], stats[:, t, :]).then_inc(moments_ready, 1)

            def normalize(n, t):
                dve.wait_ge(rstd_ready, n * NT + t + 1)
                nc.vector.tensor_scalar(xn[:, t, :], x_sb[:, t, :], meanvar[:, t, 0:1], rstd[:, t:t + 1],
                                        ALU.subtract, ALU.mult).then_inc(xn_ready, 1)

            def combine(l, t):
                dve.wait_ge(got[t], 16 * TOPK * (l + 1))
                for k in range(TOPK):
                    last = nc.vector.scalar_tensor_tensor(out=x_sb[:, t, :], in0=gathered[:, k, t, :],
                                                          scalar=topw[:, k, t:t + 1], in1=x_sb[:, t, :],
                                                          op0=ALU.mult, op1=ALU.add)
                    if k == 0:
                        settle(last)
                last.then_inc(layer_done, 1)
                dve.wait_ge(layer_done, l * NT + t + 1)

            def pass1_unit(n, unit, m):
                j, t, _, width, on_diagonal = unit
                dve.wait_ge(s1_done, n + 1)
                if n >= 2:
                    dve.wait_ge(s1_read, n - 1)
                scores = bank(pass1_bank(n)[0])[:, 0:width]
                if on_diagonal:
                    nc.vector.tensor_tensor_reduce(
                        out=dump[:, n % 2, 0:width], in0=scores, in1=mask[:, HALF - width:HALF], scale=1.0, scalar=NEG,
                        op0=ALU.add, op1=ALU.max, accum_out=rowmax[:, m, j, t:t + 1]).then_inc(s1_read, 1)
                else:
                    nc.vector.tensor_reduce(out=rowmax_a[:, m, j, t - NT // 2:t - NT // 2 + 1], in_=scores,
                                            axis=AX.X, op=ALU.max).then_inc(s1_read, 1)

            def whole_max(l, g):
                dve.wait_ge(s1_read, l * UNITS + (g + 1) * GU)
                whole = rowmax[:, g % 2, :, NT // 2:]
                nc.vector.tensor_tensor(whole, whole, rowmax_a[:, g % 2], ALU.max).then_inc(max_ready, 1)

            def copy_chunk(i, c, t):
                dve.wait_ge(stackT_done, 4 * i + c + 1)
                nc.vector.tensor_copy(chunk(c, t), chunk_bank(c)).then_inc(stackT_read[0], 1)

            def shared_inner(l, m):
                i, (_, mw) = 6 * l + m, IS_TILES[m % 3]
                dve.wait_ge(shared_silu, i + 1)
                nc.vector.tensor_tensor(hsT[0:mw, m % 3, (m // 3) * HALF:(m // 3 + 1) * HALF],
                                        silu_s[i % 2][0:mw, :], bank(4 + i % 2)[0:mw, :], ALU.mult).then_inc(shared_h, 1)

            def routing(l):
                cols = [P, NT, E]

                def wide(a):
                    return a.rearrange("p (t e) -> p t e", e=1).to_broadcast(cols)

                rev = revio[:, :, :].to_broadcast(cols)
                dve.wait_ge(logits_done, (l + 1) * NT)
                settle(nc.vector.tensor_copy(lg[:, :, :], bank(3)[:, 0:NT * E].rearrange("p (t e) -> p t e", t=NT)))
                settle(nc.vector.tensor_reduce(out=s8[:, 0, :], in_=lg[:, :, :], axis=AX.X, op=ALU.max))
                nc.vector.tensor_tensor(tmp[:, :, :], lg[:, :, :], wide(s8[:, 0, :]), ALU.subtract).then_inc(exp_in, 1)
                dve.wait_ge(exp_out, l + 1)
                settle(nc.vector.tensor_reduce(out=s8[:, 0, :], in_=ex[:, :, :], axis=AX.X, op=ALU.add))
                settle(nc.vector.reciprocal(s8[:, 1, :], s8[:, 0, :]))
                settle(nc.vector.tensor_tensor(sc[:, :, :], ex[:, :, :], wide(s8[:, 1, :]), ALU.mult))
                for k in range(TOPK):
                    settle(nc.vector.tensor_reduce(out=topw[:, k, :], in_=sc[:, :, :], axis=AX.X, op=ALU.max))
                    settle(nc.vector.tensor_tensor(tmp[:, :, :], sc[:, :, :], wide(topw[:, k, :]), ALU.is_equal))
                    settle(nc.vector.tensor_tensor(tmp[:, :, :], tmp[:, :, :], rev, ALU.mult))
                    settle(nc.vector.tensor_reduce(out=key[:, k, :], in_=tmp[:, :, :], axis=AX.X, op=ALU.max))
                    settle(nc.vector.tensor_tensor(hot[:, k], rev, wide(key[:, k, :]), ALU.is_equal))
                    if k == 0:
                        settle(nc.vector.scalar_tensor_tensor(out=sc[:, :, :], in0=hot[:, k], scalar=-4.0,
                                                              in1=sc[:, :, :], op0=ALU.mult, op1=ALU.add))
                nc.vector.tensor_tensor(hot_b[:, :, :], hot[:, 0], hot[:, 1], ALU.add).then_inc(hot_ready, 1)
                shared_inner(l, 0)
                shared_inner(l, 1)
                dve.wait_ge(rank_done, l + 1)
                ranks = bank(2)[:, 0:NT * E].rearrange("p (t e) -> p t e", t=NT)
                for k in range(TOPK):
                    settle(nc.vector.tensor_tensor(tmp[:, :, :], ranks, hot[:, k], ALU.mult))
                    settle(nc.vector.tensor_reduce(out=rank[:, k, :], in_=tmp[:, :, :], axis=AX.X, op=ALU.add))
                nc.vector.tensor_scalar(slot0[:, :, :], key[:, :, :], -float(CAP), float(E * CAP), ALU.mult, ALU.add)
                nc.vector.tensor_scalar(slot1[:, :, :], rank[:, :, :], float(CAP), float(4 * E * CAP), ALU.is_ge, ALU.mult)
                settle(nc.vector.tensor_scalar(slot2[:, :, :], rank[:, :, :], float(CAP - 1), None, ALU.min))
                nc.vector.tensor_tensor(get_at[:, :, :], slot0[:, :, :], slot2[:, :, :], ALU.add)
                settle(nc.vector.tensor_tensor(slot1[:, :, :], slot1[:, :, :], rank[:, :, :], ALU.add))
                nc.vector.tensor_tensor(put_at[:, :, :], slot0[:, :, :], slot1[:, :, :], ALU.add).then_inc(slots_known, 1)

            for l in range(LAYERS):
                for t in range(3):
                    if l > 0:
                        combine(l - 1, t)
                    moments(2 * l, t)
                    if t < 2:
                        normalize(2 * l, t)
                if l == 0:
                    dve.wait_ge(rope_loaded, 16)
                    dve.wait_ge(mask_ready, 1)
                for t in range(NT + 3):
                    units = first_units(l, t - 3) if t >= 3 else []
                    if 0 < t <= NT:
                        i = l * NT + t - 1
                        dve.wait_ge(part1_ready, i + 1)
                        r = roped[i % 3].rearrange("p (h d) -> p h d", d=HD)
                        nc.vector.tensor_tensor(r, r, parts[:, i % 3, :, 4, :], ALU.subtract).then_inc(rest_ready, 1)
                    if t + 2 < NT:
                        normalize(2 * l, t + 2)
                    if t < NT:
                        i = l * NT + t
                        dve.wait_ge(qk_done, i + 1)
                        if i >= 2:
                            dve.wait_ge(rope_sum, i - 1)
                        qk = bank(2 + i % 2).rearrange("p (h b d) -> p h b d", h=2 * NH, b=2)
                        shape = [P, 2 * NH, 2, HH]

                        def table(m):
                            return rope_sb[:, l, t, m:m + 1, :].rearrange("p o (b d) -> p o b d", b=2).to_broadcast(shape)

                        nc.vector.tensor_tensor(rope_a[i % 2].rearrange("p (h b d) -> p h b d", h=2 * NH, b=2),
                                                qk, table(0), ALU.mult)
                        nc.vector.tensor_tensor(rope_b[i % 2].rearrange("p (h b d) -> p h b d", h=2 * NH, b=2),
                                                qk[:, :, ::-1, :], table(1), ALU.mult).then_inc(rope_mul, 1)
                    if 1 < t < DVE_CHUNKS + 2:
                        copy_chunk(l * NT + t - 2, 0, t - 2)
                    for n, unit in quarter(units, 0):
                        pass1_unit(n, unit, 0)
                    for n, unit in quarter(units, 1):
                        pass1_unit(n, unit, 0)
                    if 1 < t < DVE_CHUNKS + 2:
                        copy_chunk(l * NT + t - 2, 2, t - 2)
                    for n, unit in quarter(units, 2):
                        pass1_unit(n, unit, 0)
                    if t + 3 < NT:
                        if l > 0:
                            combine(l - 1, t + 3)
                        moments(2 * l, t + 3)
                    for n, unit in quarter(units, 3):
                        pass1_unit(n, unit, 0)
                whole_max(l, 0)
                for g in range(1, NG):
                    if g > 1:
                        dve.wait_ge(s2_done, turn_of(l, g - 2) + 1)
                    for w in range((g - 1) * GU, g * GU):
                        pass1_unit(later_index(l, w), ALL_UNITS[w % GU], g % 2)
                    whole_max(l, g)
                for t in range(NT + 4):
                    if t < NT:
                        i = l * NT + t
                        dve.wait_ge(oback_done, i + 1)
                        o4 = bank(i % 2).rearrange("p (h w) -> p h w", h=NH)
                        settle(nc.vector.reciprocal(recip[:, i % 2, :], o4[:, :, HD]))
                        if i >= 2:
                            dve.wait_ge(o2T_done, i - 1)
                        nc.vector.tensor_tensor(o_tok[:, i % 2, :].rearrange("p (h d) -> p h d", h=NH), o4[:, :, 0:HD],
                                                recip[:, i % 2, :].rearrange("p (h d) -> p h d", d=1)
                                                .to_broadcast([P, NH, HD]), ALU.mult).then_inc(o_ready, 1)
                    if 3 <= t < NT + 3:
                        i = l * NT + t - 3
                        dve.wait_ge(wo_done, i + 1)
                        nc.vector.tensor_tensor(x_sb[:, t - 3, :], x_sb[:, t - 3, :], bank(4 + i % 2)[:, 0:H],
                                                ALU.add).then_inc(attn_added, 1)
                        dve.wait_ge(attn_added, i + 1)
                        moments(2 * l + 1, t - 3)
                    if t >= 4:
                        normalize(2 * l + 1, t - 4)
                routing(l)
                for m in range(2, 6):
                    shared_inner(l, m)
                for t in range(NT):
                    i = l * NT + t
                    dve.wait_ge(shared_down, i + 1)
                    nc.vector.tensor_tensor(x_sb[:, t, :], x_sb[:, t, :], bank(6 + i % 2)[:, 0:H],
                                            ALU.add).then_inc(shared_added, 1)
                for e in range(1, E + 2):
                    if e <= E:
                        i = l * E + e - 1
                        dve.wait_ge(silu_done, i + 1)
                        if i >= 2:
                            dve.wait_ge(hT_done, i - 1)
                        nc.vector.tensor_tensor(h_e[:, i % 2, :], silu_e[:, i % 2, :], bank(i % 2)[:, I:2 * I],
                                                ALU.mult).then_inc(h_ready, 1)
                    if e >= 2:
                        i = l * E + e - 2
                        dve.wait_ge(hT_done, i + 1)
                        if i >= 2:
                            dve.wait_ge(down_done, i - 1)
                        nc.vector.tensor_copy(hT_e[:, i % 2], bank(2 + i % 2)[0:IH, 0:2 * P]
                                              .rearrange("p (k s) -> p k s", k=2)).then_inc(hT_ready, 1)
                dve.wait_ge(shared_added, (l + 1) * NT)
            for t in range(NT):
                combine(LAYERS - 1, t)

        @block.tensor
        def _(pe):
            def transposes_xn(n, t, b, copied):
                pe.wait_ge(xn_ready, n * NT + t + 1)
                if copied:
                    pe.wait_ge(xnT_ready, copied)
                for k in range(KT):
                    last = nc.tensor.transpose(bank(b)[:, k * P:(k + 1) * P], xn[:, t, k * P:(k + 1) * P], ident[:, :])
                last.then_inc(xT_done, 1)

            def pass1_unit(l, g, n, unit):
                b, before = pass1_bank(n)
                j, t, first, width, _ = unit
                for half in range(2):
                    pe.wait_ge(stackT_read[half], 2 * (l * NT + t + 1))
                if n >= before:
                    pe.wait_ge(s1_read, n - before + 1)
                nc.tensor.matmul(bank(b)[:, 0:width], heads(0, g * GH + j)[0:SR, t * P:(t + 1) * P],
                                 heads(1, g * GH + j)[0:SR, first:first + width], start=True, stop=True).then_inc(s1_done, 1)

            def turn_max(l, g):
                u = turn_of(l, g)
                pe.wait_ge(max_ready, l * NG + g + 1)
                if u >= 2:
                    pe.wait_ge(s2_read, u - 1)
                nc.tensor.transpose(bank(pass2_bank(u))[0:GH * NT, 0:P], rowmax[:, g % 2].rearrange("p h t -> p (h t)"),
                                    ident[:, :]).then_inc(s2_done, 1)

            def later_unit(l, w):
                pass1_unit(l, 1 + w // GU, later_index(l, w), ALL_UNITS[w % GU])

            def pass2(l, g, s, pair):
                qc, kt = STEPS[s]
                first, width = columns(STEPS[s])
                u, q0 = use_of(l, g, s, pair), qc * HALF + first
                if u >= 2:
                    pe.wait_ge(s2_read, u - 1)
                for j in range(2):
                    h = g * GH + 2 * pair + j
                    last = nc.tensor.matmul(bank(pass2_bank(u) + j)[:, 0:width], heads(1, h)[0:SA, kt * P:(kt + 1) * P],
                                            heads(0, h)[0:SA, q0:q0 + width], start=True, stop=True)
                last.then_inc(s2_done, 1)

            def products_v(l, g, s):
                qc, kt = STEPS[s]
                first, width = columns(STEPS[s])
                n = (l * NG + g) * NS + s
                starts, ends = kt == 0, s in STEP_ENDS
                if starts and n > 0:
                    pe.wait_ge(oT_ready, (l * NG + g) * NQ + qc)
                pe.wait_ge(s2_read, use_of(l, g, s, 1) + 1)
                if diagonal(STEPS[s]):
                    pe.wait_ge(masked, 2 * ((l * NG + g) * DIAGONALS + sum(diagonal(x) for x in STEPS[:s + 1])))
                for j in range(GH):
                    last = nc.tensor.matmul(bank(7)[VW * j:VW * (j + 1), first:first + width],
                                            v_x[:, kt, g * GH + j, :], probs(n, j // 2)[:, j % 2, 0:width],
                                            start=starts, stop=ends)
                last.then_inc(pv_done, 1)

            def transposes_chunk(i, c):
                earlier = 2 * i + c // 2
                if earlier:
                    pe.wait_ge(stackT_read[c % 2], earlier)
                for h in range(8):
                    last = nc.tensor.transpose(bank(6 + c % 2)[0:SR, :].bitcast(BF16)[:, h * P:(h + 1) * P],
                                               parts[:, i % 3, 8 * c + h].rearrange("p j d -> p (j d)"), ident_b[:, :])
                last.then_inc(stackT_done, 1)

            def product_v(l, t):
                i = l * NT + t
                pe.wait_ge(wv_loaded, 16 * (l + 1))
                if i >= 1:
                    pe.wait_ge(v_copied, i)
                for k in range(KT):
                    last = nc.tensor.matmul(bank(4)[:, 0:H], xnT[:, k, t * P:(t + 1) * P],
                                            wqkv_sb[:, k, 2 * H:3 * H], start=(k == 0), stop=(k == KT - 1))
                last.then_inc(proj_done, 1)

            def back(l, t):
                i = l * NT + t
                if i >= 2:
                    pe.wait_ge(o_ready, i - 1)
                for g in range(NG):
                    last = nc.tensor.transpose(bank(i % 2)[:, g * P:(g + 1) * P], oT[:, g, t * P:(t + 1) * P], ident[:, :])
                last.then_inc(oback_done, 1)

            def o_transposes(l, t):
                i = l * NT + t
                pe.wait_ge(o_ready, i + 1)
                if i >= 1:
                    pe.wait_ge(o_T_ready, i)
                for k in range(KT):
                    last = nc.tensor.transpose(bank(2)[:, k * P:(k + 1) * P], o_tok[:, i % 2, k * P:(k + 1) * P],
                                               ident[:, :])
                last.then_inc(o2T_done, 1)

            def o_product(l, t):
                i = l * NT + t
                pe.wait_ge(o_T_ready, i + 1)
                if i >= 2:
                    pe.wait_ge(attn_added, i - 1)
                for k in range(KT):
                    last = nc.tensor.matmul(bank(4 + i % 2)[:, 0:H], o_T[:, i % 2, k, :], wo_sb[:, l, k, :],
                                            start=(k == 0), stop=(k == KT - 1))
                last.then_inc(wo_done, 1)

            def keep_clock(n, b):
                for _ in range(n):
                    nc.tensor.matmul(bank(b)[:, 0:P], ones_b[:, :], ones_b[:, :], start=True, stop=True)

            pe.wait_ge(ones_ready, 1)
            keep_clock(CLOCK_START, 7)
            pe.wait_ge(consts_ready, 1)
            for l in range(LAYERS):
                if l > 0:
                    pe.wait_ge(eo_ready, l * E)
                transposes_xn(2 * l, 0, 5, 2 * l * NT)
                pe.wait_ge(wqk_loaded, 16 * (l + 1))
                for t in range(NT + 3):
                    units = first_units(l, t - 3) if t >= 3 else []
                    if t - 3 == LAST_TILES:
                        pe.wait_ge(rope_mul, (l + 1) * NT)
                    if t < NT:
                        i = l * NT + t
                        pe.wait_ge(xnT_ready, 2 * l * NT + t + 1)
                        if i >= 2:
                            pe.wait_ge(rope_mul, i - 1)
                        for k in range(KT):
                            last = nc.tensor.matmul(bank(2 + i % 2), xnT[:, k, t * P:(t + 1) * P], wqkv_sb[:, k, 0:2 * H],
                                                    start=(k == 0), stop=(k == KT - 1))
                        last.then_inc(qk_done, 1)
                    if t <= 2:
                        product_v(l, t)
                        if t == 0:
                            transposes_xn(2 * l, 1, 5, 2 * l * NT + 1)
                        transposes_xn(2 * l, t + 2, 5, 2 * l * NT + t + 2)
                    if 1 < t <= NT + 1:
                        pe.wait_ge(parts_ready, l * NT + t - 1)
                        for c in (0, 1):
                            transposes_chunk(l * NT + t - 2, c)
                    for n, unit in quarter(units, 0):
                        pass1_unit(l, 0, n, unit)
                    for n, unit in quarter(units, 1):
                        pass1_unit(l, 0, n, unit)
                    if 1 < t <= NT + 1:
                        for c in (2, 3):
                            transposes_chunk(l * NT + t - 2, c)
                    for n, unit in quarter(units, 2):
                        pass1_unit(l, 0, n, unit)
                    if 2 < t < NT:
                        product_v(l, t)
                        if t + 2 < NT:
                            transposes_xn(2 * l, t + 2, 5, 2 * l * NT + t + 2)
                    for n, unit in quarter(units, 3):
                        pass1_unit(l, 0, n, unit)
                pe.wait_ge(rope_mul, (l + 1) * NT)
                pe.wait_ge(v_copied, (l + 1) * NT)
                pe.wait_ge(xnT_ready, (2 * l + 1) * NT)
                for w in range(EARLIEST):
                    later_unit(l, w)
                turn_max(l, 0)
                for w in range(EARLIEST, EARLY):
                    later_unit(l, w)
                pe.wait_ge(v_fixed, l + 1)
                pe.wait_ge(ones_loaded, 16 * PARTS * NG * (l + 1))
                for g in range(NG):
                    pe.wait_ge(shift_loaded, 16 * PARTS * (l * NG + g + 1))
                    for s in range(NS):
                        units = later_units(g, s)
                        if s == MAX_STEP and g + 1 < NG:
                            turn_max(l, g + 1)
                        for pair in range(2):
                            pass2(l, g, s, pair)
                            for part in range(2):
                                for w in quarter(units, 2 * pair + part):
                                    later_unit(l, w)
                        if g * NS + s >= PV_LAG:
                            products_v(l, *divmod(g * NS + s - PV_LAG, NS))
                for t, n in enumerate(range(NG * NS - PV_LAG, NG * NS)):
                    pe.wait_ge(s1_read, (l + 1) * UNITS)
                    pe.wait_ge(oT_ready, (l + 1) * NG * NQ - 1)
                    back(l, t)
                    products_v(l, *divmod(n, NS))
                if l == 0:
                    pe.wait_ge(wo_loaded, 16)
                    pe.wait_ge(moe_loaded, 64)
                for t in range(NT + 6):
                    if t == NT // 2:
                        pe.wait_ge(oT_ready, (l + 1) * NG * NQ)
                    if 2 <= t < NT:
                        back(l, t)
                    if 0 < t <= NT:
                        o_transposes(l, t - 1)
                    if 1 < t <= NT + 1:
                        o_product(l, t - 2)
                    if t > NT:
                        keep_clock(CLOCK_TAIL, 0)
                    if 5 <= t < NT + 5:
                        b = t - 5
                        transposes_xn(2 * l + 1, b, 6 + b % 2, (2 * l + 1) * NT + b - 1)
                    if t >= 6:
                        b = t - 6
                        pe.wait_ge(xnT_ready, (2 * l + 1) * NT + b + 1)
                        for k in range(KT):
                            last = nc.tensor.matmul(bank(3)[:, b * E:(b + 1) * E], xnT[:, k, b * P:(b + 1) * P],
                                                    gate_sb[:, k, :], start=(k == 0), stop=(k == KT - 1))
                        last.then_inc(logits_done, 1)

                def shared_product(m):
                    i, (m0, mw) = 6 * l + m, IS_TILES[m % 3]
                    if i >= 2:
                        pe.wait_ge(shared_h, i - 1)
                    for b, off in ((0, 0), (4, IS)):
                        for k in range(KT):
                            last = nc.tensor.matmul(bank(b + i % 2)[0:mw, :], wsgu_sb[:, k, off + m0:off + m0 + mw],
                                                    xnT[:, k, (m // 3) * HALF:(m // 3 + 1) * HALF],
                                                    start=(k == 0), stop=(k == KT - 1))
                    last.then_inc(shared_up, 1)

                shared_product(0)
                shared_product(1)
                pe.wait_ge(hot_ready, l + 1)
                nc.tensor.matmul(bank(2)[:, 0:NT * E], before[:, :], hot_b[:, :, :].rearrange("p t e -> p (t e)"),
                                 start=True, stop=False)
                for j in range(NT - 1):
                    last = nc.tensor.matmul(bank(2)[:, (j + 1) * E:NT * E].rearrange("p (t e) -> p t e", e=E),
                                            ones_b[:, :], hot_b[:, j:j + 1, :].to_broadcast([P, NT - 1 - j, E]),
                                            start=False, stop=(j == NT - 2))
                last.then_inc(rank_done, 1)
                for m in range(2, 6):
                    shared_product(m)
                for t in range(NT):
                    i = l * NT + t
                    if t == 0:
                        pe.wait_ge(shared_h, 6 * (l + 1))
                        pe.wait_ge(xnT_ready, (2 * l + 2) * NT)
                    if i >= 2:
                        pe.wait_ge(shared_added, i - 1)
                    for m, (m0, mw) in enumerate(IS_TILES):
                        last = nc.tensor.matmul(bank(6 + i % 2)[:, 0:H], hsT[0:mw, m, t * P:(t + 1) * P], wsd_sb[0:mw, m, :],
                                                start=(m == 0), stop=(m == 2))
                    last.then_inc(shared_down, 1)
                pe.wait_ge(shared_added, (l + 1) * NT)
                pe.wait_ge(slots_known, l + 1)
                for e in range(E + 3):
                    if e < E:
                        i = l * E + e
                        if e % 4 == 0:
                            pe.wait_ge(slots_loaded[e // 4], 16 * (l + 1))
                        if i >= 2:
                            pe.wait_ge(slotT_ready, i - 1)
                        for k in range(KT):
                            last = nc.tensor.transpose(bank(4 + i % 2)[:, k * P:(k + 1) * P], slots[:, e, k * P:(k + 1) * P],
                                                       ident[:, :])
                        last.then_inc(slotT_done, 1)
                    if 0 < e <= E:
                        i = l * E + e - 1
                        pe.wait_ge(slotT_ready, i + 1)
                        pe.wait_ge(expert_loaded[e - 1], 32 * (l + 1))
                        if i >= 2:
                            pe.wait_ge(h_ready, i - 1)
                        for k in range(KT):
                            last = nc.tensor.matmul(bank(i % 2)[:, 0:2 * I], slotsT[:, i % 2, k, :], wgu_sb[:, e - 1, k, :],
                                                    start=(k == 0), stop=(k == KT - 1))
                        last.then_inc(gu_done, 1)
                    if 1 < e <= E + 1:
                        i = l * E + e - 2
                        pe.wait_ge(h_ready, i + 1)
                        if i >= 2:
                            pe.wait_ge(hT_ready, i - 1)
                        for k in range(2):
                            last = nc.tensor.transpose(bank(2 + i % 2)[0:IH, k * P:(k + 1) * P],
                                                       h_e[:, i % 2, k * IH:(k + 1) * IH], ident[:, :])
                        last.then_inc(hT_done, 1)
                    if e > 2:
                        i = l * E + e - 3
                        pe.wait_ge(hT_ready, i + 1)
                        if i >= 2:
                            pe.wait_ge(eo_ready, i - 1)
                        for k in range(2):
                            last = nc.tensor.matmul(bank(6 + i % 2)[:, 0:H], hT_e[:, i % 2, k, :], wd_sb[:, e - 3, k, :],
                                                    start=(k == 0), stop=(k == 1))
                        last.then_inc(down_done, 1)


def rope_tables():
    inv_freq = (1.0 / 10000.0 ** (np.arange(0, HD, 2, dtype=np.float32) / HD)).astype(np.float32)
    freqs = np.einsum("i,j->ij", np.arange(S, dtype=np.float32), inv_freq)
    cos, sin = np.cos(freqs).astype(np.float32), np.sin(freqs).astype(np.float32)
    rows = []
    for a, b in ((cos, sin), (sin, cos)):
        rows.append(np.stack([np.concatenate([a, a], 1), np.concatenate([-b, b], 1)], 1))
    table = np.stack(rows)
    return np.ascontiguousarray(table.reshape(LAYERS, NT, P, 2, HD).transpose(2, 0, 1, 3, 4))


def kernel(**inputs):
    import numpy as _np
    import concourse.bacc as _bacc
    from concourse import mybir as _mybir
    from concourse.bass_utils import run_bass_kernel_spmd as _run

    a = {k: _np.asarray(v) for k, v in inputs.items()}

    def qkv(which):
        return _np.concatenate([a[f"L0_attn_{which}_W{m}"].T for m in "qkv"], axis=1)

    arrays = {
        "x": a["L0_attn_a_hidden_states"].reshape(S, H),
        "wqkv": _np.stack([qkv("a"), qkv("b")]),
        "wo": _np.stack([a["L0_attn_a_Wo"].T, a["L0_attn_b_Wo"].T]),
        "gate": a["L0_ffn_gate_w"].T,
        "wgu": _np.concatenate([a["L0_ffn_w_gate"], a["L0_ffn_w_up"]], axis=2),
        "wdown": a["L0_ffn_w_down"],
        "wsgu": _np.concatenate([a["L0_ffn_ws_gate"], a["L0_ffn_ws_up"]], axis=1),
        "wsdown": a["L0_ffn_ws_down"],
        "rope": rope_tables(),
    }
    nc = _bacc.Bacc("TRN2", target_bir_lowering=False, num_devices=1)
    feeds, args = {}, []
    for name, value in arrays.items():
        feeds[f"{name}_dram"] = _np.ascontiguousarray(value)
        args.append(nc.dram_tensor(f"{name}_dram", value.shape, _mybir.dt.from_np(value.dtype), kind="ExternalInput").ap())
    args.append(nc.dram_tensor("out_dram", (S, H), _mybir.dt.float32, kind="ExternalOutput").ap())
    build(nc, *args)
    r = _run(nc, [feeds], core_ids=[0])
    return r.results[0]["out_dram"].reshape(1, S, H)
```
